# Optimizing a Trainium2 kernel written in Bass

```python
import numpy as np
import jax
import jax.numpy as jnp

def _softmax(x, axis=-1):
    return jax.nn.softmax(x, axis=axis)

def _gelu(x):
    return jax.nn.gelu(x, approximate=True)

def _silu(x):
    return jax.nn.silu(x)

def _sigmoid(x):
    return jax.nn.sigmoid(x)

def _layernorm(x, axis=-1, eps=1e-05):
    m = jnp.mean(x, axis=axis, keepdims=True)
    v = jnp.var(x, axis=axis, keepdims=True)
    return (x - m) / jnp.sqrt(v + eps)

def _scatter_add(tgt, idx, src, axis=0):
    return tgt.at[idx].add(src)

def _segment_sum(src, seg, n):
    return jax.ops.segment_sum(src, seg, n)
kernel_name = 'mk_seq_preln_d1_jaxref_r4_3fdf0e'

def setup_inputs(seed: int=0):
    np.random.seed(seed)
    _w = jnp.asarray

    def _L0_attn_setup():
        import jax, jax.numpy as jnp
        import numpy as np
        B, S, D, H, DK, DL, DR = (2, 512, 512, 16, 128, 128, 64)
        EPS = 1e-06

        def _rmsnorm(x, w):
            return x * jax.lax.rsqrt(jnp.mean(x * x, axis=-1, keepdims=True) + EPS) * w

        def _rope_tables(seq_len, d):
            quarter = d // 4
            freq = (1.0 / 10000.0) ** jnp.linspace(0.0, 1.0, quarter, dtype=jnp.float32)
            freq = jnp.concatenate([freq, jnp.zeros((quarter,), jnp.float32)])
            theta = jnp.arange(seq_len, dtype=jnp.float32)[:, None] * freq[None, :]
            return (jnp.cos(theta), jnp.sin(theta))

        def _apply_rope(x, cos, sin):
            half = x.shape[-1] // 2
            x1, x2 = (x[..., :half], x[..., half:])
            c = cos[None, None, :, :]
            s = sin[None, None, :, :]
            y1 = x1 * c + x2 * s
            y2 = -x1 * s + x2 * c
            return jnp.concatenate([y1, y2], axis=-1)
        key = jax.random.key(seed)
        ks = jax.random.split(key, 9)
        w = lambda k, sh: jax.random.normal(k, sh, jnp.float32) * 0.02
        return {'x': jax.random.normal(ks[0], (B, S, D), jnp.float32), 'wq': w(ks[1], (D, H * DK)), 'w_kv_down': w(ks[2], (D, DL)), 'w_k_rope': w(ks[3], (DL, H * DR)), 'w_k_nope': w(ks[4], (DL, H * (DK - DR))), 'wv': w(ks[5], (DL, H * DK)), 'wo': w(ks[6], (H * DK, D)), 'q_norm_w': jnp.ones((DK,), jnp.float32), 'k_norm_w': jnp.ones((DK,), jnp.float32)}
    _L0_attn_in = _L0_attn_setup()

    def _L0_ffn_setup():
        import jax, jax.numpy as jnp
        import numpy as np
        from jax import lax
        E = 64
        H = 512
        I = 176
        G = 8
        TOPK_GROUP = 4
        K = 8
        B, S = (2, 512)
        N = B * S
        CAP = 2 * N * K // E
        SCALE = 2.5

        def _route(x, router_weight, e_bias):
            logits = x.astype(jnp.float32) @ router_weight.astype(jnp.float32).T
            scores = jax.nn.sigmoid(logits)
            sc = scores + e_bias
            n = x.shape[0]
            group_scores = lax.top_k(sc.reshape(n, G, E // G), 2)[0].sum(-1)
            grp_idx = lax.top_k(group_scores, TOPK_GROUP)[1]
            group_mask = jnp.zeros((n, G), jnp.float32).at[jnp.arange(n)[:, None], grp_idx].set(1.0)
            score_mask = jnp.repeat(group_mask, E // G, axis=1)
            masked = jnp.where(score_mask > 0, sc, 0.0)
            topk_idx = lax.top_k(masked, K)[1]
            topk_w = jnp.take_along_axis(scores, topk_idx, axis=1)
            topk_w = topk_w / (topk_w.sum(-1, keepdims=True) + 1e-20)
            return (topk_idx, topk_w * SCALE)

        def _moe_experts(x, topk_idx, topk_w, w_gate, w_up, w_down):
            n = x.shape[0]
            flat_e = topk_idx.reshape(-1)
            rows = jnp.repeat(jnp.arange(n), K)
            oh = jax.nn.one_hot(flat_e, E, dtype=jnp.int32)
            pos = jnp.cumsum(oh, axis=0) - oh
            pos = jnp.take_along_axis(pos, flat_e[:, None], axis=1)[:, 0]
            valid = (pos < CAP).astype(x.dtype)
            p = jnp.minimum(pos, CAP - 1)
            buf = jnp.zeros((E, CAP, H), x.dtype).at[flat_e, p].add(x[rows] * valid[:, None])
            g = jnp.einsum('ech,ehi->eci', buf, w_gate)
            u = jnp.einsum('ech,ehi->eci', buf, w_up)
            y = jnp.einsum('eci,eih->ech', jax.nn.silu(g) * u, w_down)
            y_tok = y[flat_e, p] * (topk_w.reshape(-1) * valid)[:, None]
            return jnp.zeros((n, H), x.dtype).at[rows].add(y_tok)

        def _shared_mlp(x, sh_gate, sh_up, sh_down):
            return jax.nn.silu(x @ sh_gate) * (x @ sh_up) @ sh_down
        key = jax.random.key(seed)
        ks = jax.random.split(key, 9)
        f32 = jnp.float32
        return {'hidden_states': jax.random.normal(ks[0], (B, S, H), f32), 'router_weight': jax.random.normal(ks[1], (E, H), f32) * (2.0 / H) ** 0.5, 'e_bias': jnp.zeros((E,), f32), 'w_gate': jax.random.normal(ks[2], (E, H, I), f32) * (1.0 / H) ** 0.5, 'w_up': jax.random.normal(ks[3], (E, H, I), f32) * (1.0 / H) ** 0.5, 'w_down': jax.random.normal(ks[4], (E, I, H), f32) * (1.0 / I) ** 0.5, 'sh_gate': jax.random.normal(ks[5], (H, I), f32) * (1.0 / H) ** 0.5, 'sh_up': jax.random.normal(ks[6], (H, I), f32) * (1.0 / H) ** 0.5, 'sh_down': jax.random.normal(ks[7], (I, H), f32) * (1.0 / I) ** 0.5}
    _L0_ffn_in = _L0_ffn_setup()
    _d = {'L0_attn_x': _L0_attn_in['x'], 'L0_attn_wq': _L0_attn_in['wq'], 'L0_attn_w_kv_down': _L0_attn_in['w_kv_down'], 'L0_attn_w_k_rope': _L0_attn_in['w_k_rope'], 'L0_attn_w_k_nope': _L0_attn_in['w_k_nope'], 'L0_attn_wv': _L0_attn_in['wv'], 'L0_attn_wo': _L0_attn_in['wo'], 'L0_attn_q_norm_w': _L0_attn_in['q_norm_w'], 'L0_attn_k_norm_w': _L0_attn_in['k_norm_w'], 'L0_ffn_router_weight': _L0_ffn_in['router_weight'], 'L0_ffn_e_bias': _L0_ffn_in['e_bias'], 'L0_ffn_w_gate': _L0_ffn_in['w_gate'], 'L0_ffn_w_up': _L0_ffn_in['w_up'], 'L0_ffn_w_down': _L0_ffn_in['w_down'], 'L0_ffn_sh_gate': _L0_ffn_in['sh_gate'], 'L0_ffn_sh_up': _L0_ffn_in['sh_up'], 'L0_ffn_sh_down': _L0_ffn_in['sh_down']}
    _x0 = _d['L0_attn_x']
    _d['L0_attn_x'] = jax.random.normal(jax.random.fold_in(jax.random.key(seed), 1), (4, 1024, 512), dtype=_x0.dtype)
    del _x0
    return _d

def reference(L0_attn_x, L0_attn_wq, L0_attn_w_kv_down, L0_attn_w_k_rope, L0_attn_w_k_nope, L0_attn_wv, L0_attn_wo, L0_attn_q_norm_w, L0_attn_k_norm_w, L0_ffn_router_weight, L0_ffn_e_bias, L0_ffn_w_gate, L0_ffn_w_up, L0_ffn_w_down, L0_ffn_sh_gate, L0_ffn_sh_up, L0_ffn_sh_down):

    def _L0_attn_ref(x, wq, w_kv_down, w_k_rope, w_k_nope, wv, wo, q_norm_w, k_norm_w):
        import jax, jax.numpy as jnp
        import numpy as np
        B, S, D, H, DK, DL, DR = (2, 512, 512, 16, 128, 128, 64)
        EPS = 1e-06

        def _rmsnorm(x, w):
            return x * jax.lax.rsqrt(jnp.mean(x * x, axis=-1, keepdims=True) + EPS) * w

        def _rope_tables(seq_len, d):
            quarter = d // 4
            freq = (1.0 / 10000.0) ** jnp.linspace(0.0, 1.0, quarter, dtype=jnp.float32)
            freq = jnp.concatenate([freq, jnp.zeros((quarter,), jnp.float32)])
            theta = jnp.arange(seq_len, dtype=jnp.float32)[:, None] * freq[None, :]
            return (jnp.cos(theta), jnp.sin(theta))

        def _apply_rope(x, cos, sin):
            half = x.shape[-1] // 2
            x1, x2 = (x[..., :half], x[..., half:])
            c = cos[None, None, :, :]
            s = sin[None, None, :, :]
            y1 = x1 * c + x2 * s
            y2 = -x1 * s + x2 * c
            return jnp.concatenate([y1, y2], axis=-1)
        b, s, _ = x.shape
        q = (x @ wq).reshape(b, s, H, DK)
        q = _rmsnorm(q, q_norm_w).transpose(0, 2, 1, 3)
        latent = x @ w_kv_down
        v = (latent @ wv).reshape(b, s, H, DK).transpose(0, 2, 1, 3)
        k_rope = (latent @ w_k_rope).reshape(b, s, H, DR).transpose(0, 2, 1, 3)
        k_nope = (latent @ w_k_nope).reshape(b, s, H, DK - DR).transpose(0, 2, 1, 3)
        cos, sin = _rope_tables(s, DR)
        q = jnp.concatenate([_apply_rope(q[..., :DR], cos, sin), q[..., DR:]], axis=-1)
        k = jnp.concatenate([_apply_rope(k_rope, cos, sin), k_nope], axis=-1)
        k = _rmsnorm(k, k_norm_w)
        scale = 1.0 / np.sqrt(DK).astype(np.float32)
        scores = jnp.einsum('bhqd,bhkd->bhqk', q, k) * scale
        causal = jnp.tril(jnp.ones((s, s), bool))
        scores = jnp.where(causal[None, None], scores, jnp.finfo(scores.dtype).min)
        attn = jax.nn.softmax(scores, axis=-1)
        out = jnp.einsum('bhqk,bhkd->bhqd', attn, v)
        out = out.transpose(0, 2, 1, 3).reshape(b, s, H * DK)
        return out @ wo

    def _L0_ffn_ref(hidden_states, router_weight, e_bias, w_gate, w_up, w_down, sh_gate, sh_up, sh_down):
        import jax, jax.numpy as jnp
        import numpy as np
        from jax import lax
        E = 64
        H = 512
        I = 176
        G = 8
        TOPK_GROUP = 4
        K = 8
        B, S = (2, 512)
        N = B * S
        CAP = 2 * N * K // E
        SCALE = 2.5

        def _route(x, router_weight, e_bias):
            logits = x.astype(jnp.float32) @ router_weight.astype(jnp.float32).T
            scores = jax.nn.sigmoid(logits)
            sc = scores + e_bias
            n = x.shape[0]
            group_scores = lax.top_k(sc.reshape(n, G, E // G), 2)[0].sum(-1)
            grp_idx = lax.top_k(group_scores, TOPK_GROUP)[1]
            group_mask = jnp.zeros((n, G), jnp.float32).at[jnp.arange(n)[:, None], grp_idx].set(1.0)
            score_mask = jnp.repeat(group_mask, E // G, axis=1)
            masked = jnp.where(score_mask > 0, sc, 0.0)
            topk_idx = lax.top_k(masked, K)[1]
            topk_w = jnp.take_along_axis(scores, topk_idx, axis=1)
            topk_w = topk_w / (topk_w.sum(-1, keepdims=True) + 1e-20)
            return (topk_idx, topk_w * SCALE)

        def _moe_experts(x, topk_idx, topk_w, w_gate, w_up, w_down):
            n = x.shape[0]
            flat_e = topk_idx.reshape(-1)
            rows = jnp.repeat(jnp.arange(n), K)
            oh = jax.nn.one_hot(flat_e, E, dtype=jnp.int32)
            pos = jnp.cumsum(oh, axis=0) - oh
            pos = jnp.take_along_axis(pos, flat_e[:, None], axis=1)[:, 0]
            valid = (pos < CAP).astype(x.dtype)
            p = jnp.minimum(pos, CAP - 1)
            buf = jnp.zeros((E, CAP, H), x.dtype).at[flat_e, p].add(x[rows] * valid[:, None])
            g = jnp.einsum('ech,ehi->eci', buf, w_gate)
            u = jnp.einsum('ech,ehi->eci', buf, w_up)
            y = jnp.einsum('eci,eih->ech', jax.nn.silu(g) * u, w_down)
            y_tok = y[flat_e, p] * (topk_w.reshape(-1) * valid)[:, None]
            return jnp.zeros((n, H), x.dtype).at[rows].add(y_tok)

        def _shared_mlp(x, sh_gate, sh_up, sh_down):
            return jax.nn.silu(x @ sh_gate) * (x @ sh_up) @ sh_down
        orig_shape = hidden_states.shape
        x = hidden_states.reshape(-1, H)
        topk_idx, topk_w = _route(x, router_weight, e_bias)
        moe_out = _moe_experts(x, topk_idx, topk_w.astype(x.dtype), w_gate, w_up, w_down)
        out = moe_out + _shared_mlp(x, sh_gate, sh_up, sh_down)
        return out.reshape(orig_shape)
    x = L0_attn_x
    x = x + _L0_attn_ref(_layernorm(x, axis=-1), L0_attn_wq, L0_attn_w_kv_down, L0_attn_w_k_rope, L0_attn_w_k_nope, L0_attn_wv, L0_attn_wo, L0_attn_q_norm_w, L0_attn_k_norm_w)
    x = x + _L0_ffn_ref(_layernorm(x, axis=-1), L0_ffn_router_weight, L0_ffn_e_bias, L0_ffn_w_gate, L0_ffn_w_up, L0_ffn_w_down, L0_ffn_sh_gate, L0_ffn_sh_up, L0_ffn_sh_down)
    return x

_drawn_inputs = setup_inputs


def setup_inputs(seed=0):
    import zlib

    import numpy as np

    out = dict(_drawn_inputs(seed))
    spreads = {'L0_attn_q_norm_w': (1.0, 0.584),
     'L0_attn_k_norm_w': (1.0, 0.6),
     'L0_ffn_e_bias': (0.0, 0.1)}
    factors = {}
    for name, (base, spread) in spreads.items():
        noise = np.random.default_rng([zlib.crc32(name.encode()), seed]).standard_normal(out[name].shape)
        drawn = base * np.exp(spread * noise) if base else spread * noise
        out[name] = jnp.asarray(drawn.astype(out[name].dtype))
    for name, factor in factors.items():
        out[name] = (out[name] * factor).astype(out[name].dtype)
    return out
```

```python
import concourse.bass as bass
from concourse import mybir
from contextlib import ExitStack

F32, F32R, BF16 = mybir.dt.float32, mybir.dt.float32r, mybir.dt.bfloat16
I32, U32 = mybir.dt.int32, mybir.dt.uint32
ACT = mybir.ActivationFunctionType
ALU = mybir.AluOpType
AX = mybir.AxisListType

P = 128
BANK = 512
BATCH, SEQ, DIM = 4, 1024, 512
HEADS, DK, DLAT, DROPE = 16, 128, 128, 64
TILES = SEQ // P
CHUNKS = DIM // P
PAIR = 2
GROUPS = HEADS // PAIR
GW = PAIR * DK
ROT = DROPE // 4
HALF = DROPE // 2
STEPS = PAIR * TILES
EPS_LN, EPS_RMS = 1e-5, 1e-6
MASKED = -1e30
TOKENS = BATCH * SEQ
EXPERTS, INNER, EGROUPS, TOPG, TOPK = 64, 176, 8, 4, 8
EG = EXPERTS // EGROUPS
CAP = 2 * 1024 * TOPK // EXPERTS
CHALF = CAP // P
SCALE_ROUTE = 2.5
TAIL = INNER - P
GU = 3 * P
QUAD = 4
SLOTS = EXPERTS * CAP
NEWTON = 3


def build(nc, a, out):
    def dram(name, shape, dt=F32):
        return nc.dram_tensor(name, shape, dt, kind="Internal").ap()

    wqk_split = dram("wqk_split", (GROUPS, P, 2, CHUNKS + 1, GW))
    wvo_split = dram("wvo_split", (GROUPS, P, 2, PAIR, DIM))
    xn_rows = dram("xn_rows", (TOKENS + CAP, DIM))
    sum_rows = dram("sum_rows", (TOKENS + CAP, DIM))
    slot_table = dram("slot_table", (SLOTS, 2), I32)

    outer = ExitStack()
    with outer:
        sems = {}

        def sem(name):
            if name not in sems:
                sems[name] = outer.enter_context(nc.semaphore(name))
            return sems[name]

        def sb(stack, name, shape, dt=F32):
            return stack.enter_context(nc.sbuf_tensor(name, shape, dt))

        ident = sb(outer, "ident", [P, P])
        ident_b = sb(outer, "ident_b", [P, P], BF16)
        kvd = sb(outer, "kvd", [P, 2, CHUNKS, DLAT], F32R)
        wq_col = sb(outer, "wq_col", [P, 1])
        newton = sb(outer, "newton", [P, 2])
        banks = [outer.enter_context(nc.psum_tensor(f"bank{i}", [P, BANK], F32)) for i in range(4)]
        psS = outer.enter_context(nc.psum_tensor("psS", [P, 2, 2 * BANK], F32))
        psT, psX = banks[0:2], banks[2:4]

        def mm3(dst, left, right, start, stop):
            (lh, ll), (rh, rl) = left, right
            nc.tensor.matmul(dst, lh, rh, start=start, stop=False)
            nc.tensor.matmul(dst, lh, rl, start=False, stop=False)
            return nc.tensor.matmul(dst, ll, rh, start=False, stop=stop)

        def rsqrt(dve, s, n, v, y, t, last=None):
            k = [0]

            def after(ins):
                k[0] += 1
                ins.then_inc(s, 1)
                dve.wait_ge(s, n + k[0])

            after(nc.vector.tensor_scalar(t.bitcast(I32), v.bitcast(I32), 1, None, ALU.logical_shift_right))
            after(nc.vector.tensor_scalar(y.bitcast(I32), t.bitcast(I32), -1.0, float(0x5F3759DF), ALU.mult, ALU.add))
            for _ in range(NEWTON):
                after(nc.vector.tensor_tensor(t, y, y, ALU.mult))
                after(nc.vector.scalar_tensor_tensor(t, t, -0.5, v, ALU.mult, ALU.mult))
                after(nc.vector.scalar_tensor_tensor(y, t, 1.5, y, ALU.add, ALU.mult))
            return k[0]

        RSQRT_OPS = 2 + 3 * NEWTON

        prepare(nc, a, sem, sb, outer, dict(
            ident=ident, ident_b=ident_b, kvd=kvd, wq_col=wq_col, newton=newton, wqk_split=wqk_split,
            wvo_split=wvo_split, banks=banks, psS=psS))
        gu_split = dram("gu_split", (P, 2, CHUNKS, GU))
        dn_split = dram("dn_split", (P, 2, 2, DIM))
        rt_split = dram("rt_split", (P, 2, CHUNKS, EXPERTS))
        scratch = dict(xn_rows=xn_rows, sum_rows=sum_rows, slot_table=slot_table, gu_split=gu_split, dn_split=dn_split,
                       rt_split=rt_split, ident=ident, banks=banks, psT=psT, psX=psX, psS=psS)
        split_ffn(nc, a, sem, sb, scratch)
        with ExitStack() as layers:
            acc = sb(layers, "acc", [P, TILES, DIM])
            rope = sb(layers, "rope", [P, 4, TILES, 2 * PAIR, ROT])
            causal = sb(layers, "causal", [P, P], BF16)
            rope_tables(nc, a, sem, sb, rope, causal)
            routing = dict(
                scratch, acc=acc,
                seen=sb(layers, "seen", [P, EXPERTS], BF16),
                token=sb(layers, "token", [P, QUAD]),
                lower=sb(layers, "lower", [P, EGROUPS, EGROUPS]),
                before=sb(layers, "before", [P, P], BF16),
                ones=sb(layers, "ones", [P, P], BF16),
                number=sb(layers, "number", [P, EXPERTS]),
                number2=sb(layers, "number2", [P, EXPERTS]),
                bias_row=sb(layers, "bias_row", [P, EXPERTS]),
                table_row=sb(layers, "table_row", [P, QUAD, TOPK], I32),
                entry=sb(layers, "entry", [P, QUAD, TOPK, 2], I32))
            routing_constants(nc, a, sem, routing)
            with nc.Fori(0, BATCH) as b:
                with ExitStack() as st:
                    attend(nc, a, b, sem, sb, st, mm3, rsqrt, RSQRT_OPS, dict(
                        ident=ident, ident_b=ident_b, kvd=kvd, wq_col=wq_col, newton=newton, wqk_split=wqk_split,
                        wvo_split=wvo_split, psT=psT, psX=psX, psS=psS, acc=acc, rope=rope, causal=causal))
                with ExitStack() as st:
                    route(nc, a, b, sem, sb, st, mm3, rsqrt, RSQRT_OPS, routing)
        with ExitStack() as st:
            experts(nc, a, sem, sb, st, mm3, scratch)
        finish(nc, sem, out, sum_rows)


def holder(sem):
    passed = sem("passed")

    def hold(eng, s, value):
        eng.wait_ge(s, value)
        if not isinstance(value, int):
            eng.sem_inc(passed, 1)
    return hold


def gu_views(part, raw):
    return [(part[:, :, 0:2 * P].rearrange("p c (w n) -> p c w n", w=2), raw[:, :, :, 0:P]),
            (part[:, :, 2 * P:GU].rearrange("p c (w n) -> p c w n", w=2)[:, :, :, 0:TAIL], raw[:, :, :, P:INNER])]


def prepare(nc, a, sem, sb, outer, m):
    ident, ident_b, kvd, wq_col, banks = m["ident"], m["ident_b"], m["kvd"], m["wq_col"], m["banks"]
    ident_set, ident_b_set, kv_in, kv_high = sem("ident_set"), sem("ident_b_set"), sem("kv_in"), sem("kv_high")
    col_in, col_ones, col_set = sem("col_in"), sem("col_ones"), sem("col_set")
    wide_in = [sem("wide_in0"), sem("wide_in1")]
    wide_high, wide_low = sem("wide_high"), sem("wide_low")
    wide_out = [sem("wide_out0"), sem("wide_out1")]
    wv_in, wo_in = sem("wv_in"), [sem("wo_in0"), sem("wo_in1")]
    wv_turned, wv_copied, vo_made, vo_high, vo_low = sem("wv_turned"), sem("wv_copied"), sem("vo_made"), sem("vo_high"), sem("vo_low")
    vo_out = [sem("vo_out0"), sem("vo_out1")]
    wide = HEADS * DK
    with ExitStack() as st:
        kv_raw = sb(st, "kv_raw", [P, CHUNKS, DLAT])
        raw = sb(st, "raw", [P, 2, wide])
        part = sb(st, "part", [P, 2, 2, wide], F32R)
        cols = sb(st, "cols", [P, 2])
        wv_raw = sb(st, "wv_raw", [P, wide])
        wo_raw = sb(st, "wo_raw", [P, 2, DIM])
        wv_t = sb(st, "wv_t", [P, 2, DLAT])
        vo = sb(st, "vo", [P, 2, 2, DIM], F32R)
        block = st.enter_context(nc.Block())

        @block.gpsimd
        def _(pool):
            nc.gpsimd.memset(ident[:], 0.0).then_inc(ident_set, 1)
            nc.gpsimd.memset(ident_b[:], 0.0).then_inc(ident_set, 1)
            nc.gpsimd.memset(m["newton"][:, 0:1], -0.5)
            nc.gpsimd.memset(m["newton"][:, 1:2], 1.5)
            pool.wait_ge(ident_set, 2)
            for i in (ident, ident_b):
                nc.gpsimd.affine_select(out=i[:], in_=i[:], compare_op=ALU.not_equal, fill=1.0, base=0,
                                        pattern=[[-1, P]], channel_multiplier=1).then_inc(ident_b_set, 1)

        @block.sync
        def _(sp):
            sp.dma_start(kv_raw[:], a["w_kv_down"].rearrange("(c p) n -> p c n", p=P)).then_inc(kv_in, 16)
            sp.dma_start(cols[:, 0:1], a["q_norm_w"].rearrange("(p o) -> p o", o=1)).then_inc(col_in, 16)
            sp.dma_start(cols[:, 1:2], a["k_norm_w"].rearrange("(p o) -> p o", o=1)).then_inc(col_in, 16)
            sp.dma_start(wv_raw[:], a["wv"]).then_inc(wv_in, 16)
            for c in range(CHUNKS + 1):
                k = c % 2
                if c >= 2:
                    sp.wait_ge(wide_low, c - 1)
                if c < CHUNKS:
                    sp.dma_start(raw[:, k, :], a["wq"][c * P:(c + 1) * P, :]).then_inc(wide_in[k], 16)
                else:
                    r = raw[:, k, :].rearrange("p (h n) -> p h n", n=DK)
                    sp.dma_start(r[:, :, 0:DROPE], a["w_k_rope"].rearrange("p (h n) -> p h n", n=DROPE)).then_inc(wide_in[k], 16)
                    sp.dma_start(r[:, :, DROPE:DK], a["w_k_nope"].rearrange("p (h n) -> p h n", n=DK - DROPE)).then_inc(wide_in[k], 16)
            for h in range(HEADS):
                if h >= 2:
                    sp.wait_ge(vo_made, h - 1)
                sp.dma_start(wo_raw[:, h % 2, :], a["wo"][h * DK:(h + 1) * DK, :]).then_inc(wo_in[h % 2], 16)

        @block.scalar
        def _(act):
            act.wait_ge(kv_in, 16)
            nc.scalar.activation(kvd[:, 0, :, :], kv_raw[:], ACT.Copy).then_inc(kv_high, 1)
            for c in range(CHUNKS + 1):
                k = c % 2
                act.wait_ge(wide_in[k], 16 * (c // 2 + 1) + (16 if c == CHUNKS else 0))
                if c >= 2:
                    act.wait_ge(wide_out[k], 32 * (c // 2))
                nc.scalar.activation(part[:, k, 0, :], raw[:, k, :], ACT.Copy).then_inc(wide_high, 1)
                act.wait_ge(wide_low, c + 1)
                act.wait_ge(wide_high, c + 1)
                for s in range(2):
                    act.dma_start(m["wqk_split"][:, :, s, c, :].rearrange("g p n -> p g n"),
                                  part[:, k, s, :].bitcast(F32).rearrange("p (g n) -> p g n", n=GW)).then_inc(wide_out[k], 16)
            for h in range(HEADS):
                k = h % 2
                act.wait_ge(wv_turned, h + 1)
                if h >= 2:
                    act.wait_ge(vo_made, h - 1)
                nc.scalar.activation(wv_t[:, k, :], banks[k][:, 0:DLAT], ACT.Copy).then_inc(wv_copied, 1)
                act.wait_ge(vo_made, h + 1)
                if h >= 2:
                    act.wait_ge(vo_out[k], 16 * (h // 2))
                nc.scalar.activation(vo[:, k, 0, :], banks[2 + k][:], ACT.Copy).then_inc(vo_high, 1)
                act.wait_ge(vo_low, h + 1)
                act.dma_start(m["wvo_split"][h // PAIR, :, :, h % PAIR, :], vo[:, k, :, :].bitcast(F32)).then_inc(vo_out[k], 16)
            for k in range(2):
                act.wait_ge(wide_out[k], 32 * ((CHUNKS + 2 - k) // 2))
                act.wait_ge(vo_out[k], 16 * (HEADS // 2))

        @block.vector
        def _(dve):
            dve.wait_ge(kv_high, 1)
            nc.vector.tensor_tensor(kvd[:, 1, :, :], kv_raw[:], kvd[:, 0, :, :].bitcast(F32), ALU.subtract)
            dve.wait_ge(col_in, 32)
            nc.vector.memset(cols[0:ROT, 0:1], 1.0).then_inc(col_ones, 1)
            nc.vector.memset(cols[HALF:HALF + ROT, 0:1], 1.0).then_inc(col_ones, 1)
            dve.wait_ge(col_ones, 2)
            nc.vector.scalar_tensor_tensor(wq_col[:], cols[:, 0:1], float(DK) ** -0.5, cols[:, 1:2], ALU.mult, ALU.mult).then_inc(col_set, 1)
            for c in range(CHUNKS + 1):
                k = c % 2
                dve.wait_ge(wide_high, c + 1)
                nc.vector.tensor_tensor(part[:, k, 1, :], raw[:, k, :], part[:, k, 0, :].bitcast(F32),
                                        ALU.subtract).then_inc(wide_low, 1)
            for h in range(HEADS):
                k = h % 2
                dve.wait_ge(vo_high, h + 1)
                nc.vector.tensor_tensor(vo[:, k, 1, :], banks[2 + k][:], vo[:, k, 0, :].bitcast(F32),
                                        ALU.subtract).then_inc(vo_low, 1)

        @block.tensor
        def _(pe):
            pe.wait_ge(ident_b_set, 1)
            pe.wait_ge(wv_in, 16)
            for h in range(HEADS):
                k = h % 2
                if h >= 2:
                    pe.wait_ge(wv_copied, h - 1)
                nc.tensor.transpose(banks[k][:, 0:DLAT], wv_raw[:, h * DK:(h + 1) * DK], ident[:]).then_inc(wv_turned, 1)
                pe.wait_ge(wv_copied, h + 1)
                pe.wait_ge(wo_in[k], 16 * (h // 2 + 1))
                if h >= 2:
                    pe.wait_ge(vo_low, h - 1)
                nc.tensor.matmul(banks[2 + k][:], wv_t[:, k, :], wo_raw[:, k, :], start=True, stop=True).then_inc(vo_made, 1)


def rope_tables(nc, a, sem, sb, rope, causal):
    trig_in, tables_set, causal_set = sem("trig_in"), sem("tables_set"), sem("causal_set")
    with ExitStack() as st:
        trig = sb(st, "trig", [P, 2, TILES, ROT])
        qw_row = sb(st, "qw_row", [P, DK])
        block = st.enter_context(nc.Block())

        @block.sync
        def _(sp):
            sp.dma_start(trig[:, 0], a["rope_cos"].rearrange("(t p) n -> p t n", p=P)).then_inc(trig_in, 16)
            sp.dma_start(trig[:, 1], a["rope_sin"].rearrange("(t p) n -> p t n", p=P)).then_inc(trig_in, 16)
            sp.dma_start(qw_row[:], a["q_norm_w"].rearrange("(o n) -> o n", o=1).to_broadcast([P, DK])).then_inc(trig_in, 16)

        @block.vector
        def _(dve):
            dve.wait_ge(trig_in, 48)
            for table, which, first in ((0, 0, 0), (1, 1, HALF), (2, 0, HALF), (3, 1, 0)):
                w = qw_row[:, first:first + ROT].unsqueeze(1).to_broadcast([P, TILES, ROT])
                for slot in range(2 * PAIR):
                    if slot < PAIR:
                        nc.vector.tensor_tensor(rope[:, table, :, slot, :], trig[:, which], w, ALU.mult)
                    else:
                        nc.vector.tensor_copy(rope[:, table, :, slot, :], trig[:, which])

        @block.gpsimd
        def _(pool):
            nc.gpsimd.memset(causal[:], 0.0).then_inc(causal_set, 1)
            pool.wait_ge(causal_set, 1)
            nc.gpsimd.affine_select(out=causal[:], in_=causal[:], compare_op=ALU.is_ge, fill=MASKED, base=0,
                                    pattern=[[-1, P]], channel_multiplier=1)


def attend(nc, a, b, sem, sb, st, mm3, rsqrt, RSQRT_OPS, m):
    ident, ident_b, kvd, wq_col = m["ident"], m["ident_b"], m["kvd"], m["wq_col"]
    psT, psX, psS, acc, rope, causal = m["psT"], m["psX"], m["psS"], m["acc"], m["rope"], m["causal"]
    hold = holder(sem)
    newton = m["newton"]
    WIDTH = [5, 6, 7, 8]
    xnT = sb(st, "xnT", [P, 2, CHUNKS, SEQ], F32R)
    latT = sb(st, "latT", [P, 2, SEQ], F32R)
    lat = sb(st, "lat", [P, 2, TILES, DLAT], F32R)
    qk = sb(st, "qk", [P, TILES, 2 * PAIR, DK])
    sq = sb(st, "sq", [P, 2 * PAIR, DK])
    ss = sb(st, "ss", [P, TILES, 2 * PAIR])
    rn = sb(st, "rn", [P, TILES, 2 * PAIR])
    qT = sb(st, "qT", [P, 2, 2, SEQ], F32R)
    kT = sb(st, "kT", [P, 2, 2, SEQ], F32R)
    wqk = sb(st, "wqk", [P, 2, CHUNKS + 1, GW], F32R)
    wvo = sb(st, "wvo", [P, 2, PAIR, DIM], F32R)
    attnT = sb(st, "attnT", [P, 2, PAIR, SEQ], F32R)
    probs = [sb(st, f"probs{i}", [P, w * P]) for i, w in enumerate(WIDTH)]
    pT = [sb(st, f"pT{i}", [P, 2, 2 * (i + 1 + 2) , 2 * P], F32R) for i in range(2)]
    prod = sb(st, "prod", [P, 2, 4 * 2 * PAIR, ROT])
    newt = sb(st, "newt", [P, 3, 4 * 2 * PAIR])
    nmax = sb(st, "nmax", [P, 4])
    bias = sb(st, "bias", [P, 4])
    rsum = sb(st, "rsum", [P, 4])
    rinv = sb(st, "rinv", [P, 4])
    stats = sb(st, "stats", [P, TILES, 6])
    mv = sb(st, "mv", [P, TILES, 2])
    rstd = sb(st, "rstd", [P, TILES])
    xn = [probs[2], probs[3]]

    x_in = [sem(f"x_in{i}") for i in range(4)]
    S = {n: sem(n) for n in (
        "ln_stats", "ln_mean", "ln_var", "ln_rsqrt", "xn_made", "xn_turned", "xnT_high", "xnT_low",
        "lat_made", "latT_high", "latT_low", "lat_turned", "lat_high", "lat_low",
        "wqk_in", "wvo_in", "projected", "squared", "qk_copied", "sq_summed", "rope_prod", "rope_done",
        "ms_made", "ms_halved", "seeded", "newton_chain", "rn_made", "k_normed", "qk_turned", "qkT_high", "qkT_low",
        "scored", "max_made", "bias_made", "exped", "rinv_made", "normed", "p_turned", "pT_high", "pT_low",
        "valued", "attn_high", "attn_low", "rows_made", "rows_added")}
    CHUNK = [0]
    for n in range(STEPS):
        CHUNK.append(CHUNK[-1] + (n % TILES) // 4 + 1)
    NCH = CHUNK[-1]
    OUT_AT = {0: [0], 1: [1, 2], 2: [3], 3: [4], 4: [5], 5: [6, 7]}
    PROJ_AT = {6 + t: [t] for t in range(TILES)}
    TURN_AT = {0: (0, 0, 2), 2: (0, 0, 3), 4: (0, 1, 0), 6: (0, 1, 1), 8: (0, 1, 2), 10: (0, 1, 3), 12: (1, 0, 0), 14: (1, 0, 1)}
    PAIRS = TILES // 2
    BANK_OF = {}
    for n in range(STEPS):
        tasks = [("values", (n // 2 - 1) % (2 * PAIRS))] if n % 2 else []
        tasks += [("rows", t) for t in OUT_AT.get(n, [])] + [("project", t) for t in PROJ_AT.get(n, [])]
        tasks += [("turn",) + TURN_AT[n][1:]] if n in TURN_AT else []
        for task in tasks:
            BANK_OF[task] = len(BANK_OF) % 2
    block = st.enter_context(nc.Block())

    def groups(eng, body):
        body(b * GROUPS, True, False)
        with eng.Fori(1, GROUPS - 1) as g:
            body(b * GROUPS + g, False, False)
        body(b * GROUPS + (GROUPS - 1), False, True)

    @block.sync
    def _(sp):
        x_b = a["x"][b].rearrange("(t p) d -> p t d", p=P)
        sp.dma_start(wqk[:].bitcast(F32), m["wqk_split"][0]).then_inc(S["wqk_in"], 16)
        for i in range(4):
            sp.dma_start(acc[:, 2 * i:2 * i + 2, :], x_b[:, 2 * i:2 * i + 2, :]).then_inc(x_in[i], 16)

        def body(g, G, first, last):
            if not last:
                sp.wait_ge(S["projected"], (G + 1) * TILES)
                sp.dma_start(wqk[:].bitcast(F32), m["wqk_split"][bass.ds(g + 1, 1)].squeeze(0)).then_inc(S["wqk_in"], 16)
            if not first:
                sp.wait_ge(S["rows_made"], G * TILES)
            sp.dma_start(wvo[:].bitcast(F32), m["wvo_split"][bass.ds(g, 1)].squeeze(0)).then_inc(S["wvo_in"], 16)

        body(0, b * GROUPS, True, False)
        with sp.Fori(1, GROUPS - 1) as g:
            body(g, b * GROUPS + g, False, False)
        body(GROUPS - 1, b * GROUPS + (GROUPS - 1), False, True)

    @block.gpsimd
    def _(pool):
        def newton_steps(G, half):
            v, minus_half, t = newt[:, 0], newt[:, 2], newt[:, 1]
            y = rn[:, 4 * half:4 * half + 4].rearrange("p t s -> p (t s)")
            c = [newton[:, i:i + 1].to_broadcast([P, 4 * 2 * PAIR]) for i in range(2)]
            pool.wait_ge(S["seeded"], 2 * G + half + 1)
            ops = [(minus_half, v, c[0], ALU.mult)] + NEWTON * [
                (t, y, y, ALU.mult), (t, t, minus_half, ALU.mult), (t, t, c[1], ALU.add), (y, y, t, ALU.mult)]
            for i, (dst, left, right, op) in enumerate(ops):
                if i:
                    pool.wait_ge(S["newton_chain"], (2 * G + half) * (len(ops) - 1) + i)
                done = S["newton_chain"] if i + 1 < len(ops) else S["rn_made"]
                nc.gpsimd.tensor_tensor(dst, left, right, op).then_inc(done, 1)

        def norm_k(G, half):
            newton_steps(G, half)
            pool.wait_ge(S["rope_done"], 4 * G + 2 * half + 2)
            pool.wait_ge(S["rn_made"], 2 * G + half + 1)
            k = qk[:, 4 * half:4 * half + 4, PAIR:2 * PAIR, :]
            r = rn[:, 4 * half:4 * half + 4, PAIR:2 * PAIR].unsqueeze(3).to_broadcast([P, 4, PAIR, DK])
            nc.gpsimd.tensor_tensor(k, k, r, ALU.mult).then_inc(S["k_normed"], 1)

        def norm_p(G, n):
            t = n % TILES
            p = probs[n % 4][:, 0:(t + 1) * P]
            pool.wait_ge(S["rinv_made"], STEPS * G + n + 1)
            nc.gpsimd.tensor_tensor(p, p, rinv[:, n % 4:n % 4 + 1].to_broadcast([P, (t + 1) * P]), ALU.mult).then_inc(S["normed"], 1)

        def body(G, first, last):
            for n in range(STEPS):
                if n + 2 < STEPS:
                    norm_p(G, n + 2)
                elif not last:
                    norm_p(G + 1, n + 2 - STEPS)
                if n == 9 and not last:
                    norm_k(G + 1, 0)
                if n == 13 and not last:
                    norm_k(G + 1, 1)

        norm_k(b * GROUPS, 0)
        norm_k(b * GROUPS, 1)
        norm_p(b * GROUPS, 0)
        norm_p(b * GROUPS, 1)
        groups(pool, body)

    @block.scalar
    def _(act):
        def copy_proj(G, t, bank, opening=False):
            act.wait_ge(S["projected"], TILES * G + t + 1)
            if not (opening and t == 0):
                act.wait_ge(S["sq_summed"], TILES * G + t)
            nc.scalar.activation(sq[:].rearrange("p s n -> p (s n)"), bank[:], ACT.Square).then_inc(S["squared"], 1)
            if not opening:
                act.wait_ge(S["qk_turned"], 2 * PAIRS * G - PAIRS + t // 2 + 1)
            nc.scalar.activation(qk[:, t].rearrange("p s n -> p (s n)"), bank[:], ACT.Copy).then_inc(S["qk_copied"], 1)

        def high_turned(G, h, pair):
            u = 2 * PAIRS * G + PAIRS * h + pair
            at = slice(2 * pair * P, (2 * pair + 2) * P)
            act.wait_ge(S["qk_turned"], u + 1)
            bank = psX[BANK_OF["turn", h, pair]]
            nc.scalar.activation(qT[:, h, 0, at], bank[:, 0:2 * P], ACT.Copy, scale=wq_col[:, 0:1]).then_inc(S["qkT_high"], 1)
            nc.scalar.activation(kT[:, h, 0, at], bank[:, 2 * P:4 * P], ACT.Copy).then_inc(S["qkT_high"], 1)

        def exp(G, n, opening=False):
            t = n % TILES
            act.wait_ge(S["bias_made"], STEPS * G + n + 1)
            if n >= 4:
                act.wait_ge(S["p_turned"], NCH * G + CHUNK[n - 3])
            elif not opening:
                act.wait_ge(S["p_turned"], NCH * G - NCH + CHUNK[n + 13])
            nc.scalar.activation(probs[n % 4][:, 0:(t + 1) * P], psS[:, n % 2, 0:(t + 1) * P], ACT.Exp,
                                 bias=bias[:, n % 4:n % 4 + 1], scale=rn[:, t, n // TILES:n // TILES + 1],
                                 accum_out=rsum[:, n % 4:n % 4 + 1]).then_inc(S["exped"], 1)

        def high_values(G, u):
            h, pair = u // PAIRS, u % PAIRS
            act.wait_ge(S["valued"], 2 * PAIRS * G + u + 1)
            nc.scalar.activation(attnT[:, 0, h, 2 * pair * P:(2 * pair + 2) * P], psX[BANK_OF["values", u]][:, 0:2 * P],
                                 ACT.Copy).then_inc(S["attn_high"], 1)

        def high_probs(G, n, opening):
            t = n % TILES
            u = n // 2
            if u >= 2:
                act.wait_ge(S["valued"], 2 * PAIRS * G + u - 1)
            elif not opening:
                act.wait_ge(S["valued"], 2 * PAIRS * G - 1 + u)
            for c in range(t // 4 + 1):
                act.wait_ge(S["p_turned"], NCH * G + CHUNK[n] + c + 1)
                k = min(4, t + 1 - 4 * c)
                nc.scalar.activation(pT[u % 2][:, 0, 4 * c:4 * c + k, (n % 2) * P:(n % 2 + 1) * P],
                                     psT[c][:, 0:k * P].rearrange("p (j q) -> p j q", q=P), ACT.Copy).then_inc(S["pT_high"], 1)

        def body(G, first, last):
            for n in range(STEPS):
                if n + 2 < STEPS:
                    exp(G, n + 2, first)
                elif not last:
                    exp(G + 1, n + 2 - STEPS)
                if n % 2 and not (first and n == 1):
                    high_values(G, n // 2 - 1) if n > 1 else high_values(G - 1, 2 * PAIRS - 1)
                for t in PROJ_AT.get(n, []) if not last else []:
                    copy_proj(G + 1, t, psX[BANK_OF["project", t]])
                if n in TURN_AT:
                    ahead, h, pair = TURN_AT[n]
                    if not (ahead and last):
                        high_turned(G + ahead, h, pair)
                high_probs(G, n, first)

        for t in range(TILES):
            act.wait_ge(S["xn_turned"], TILES * b + t + 1)
            nc.scalar.activation(xnT[:, 0, :, t * P:(t + 1) * P], psT[t % 2][:].rearrange("p (c q) -> p c q", q=P),
                                 ACT.Copy).then_inc(S["xnT_high"], 1)
        for q in range(2):
            act.wait_ge(S["lat_made"], 2 * b + q + 1)
            nc.scalar.activation(latT[:, 0, q * BANK:(q + 1) * BANK], psX[q][:], ACT.Copy).then_inc(S["latT_high"], 1)
        for q in range(2):
            act.wait_ge(S["lat_turned"], 4 * b + 2 * q + 1)
            nc.scalar.activation(lat[:, 0, 4 * q:4 * q + 4, :], psT[0][:].rearrange("p (j n) -> p j n", n=P),
                                 ACT.Copy).then_inc(S["lat_high"], 1)
        G0 = b * GROUPS
        for t in range(TILES):
            copy_proj(G0, t, psX[t % 2], opening=True)
        high_turned(G0, 0, 0)
        high_turned(G0, 0, 1)
        exp(G0, 0, opening=True)
        exp(G0, 1, opening=True)
        groups(act, body)
        high_values(G0 + (GROUPS - 1), 2 * PAIRS - 1)

    @block.vector
    def _(dve):
        def sum_squares(G, t):
            dve.wait_ge(S["squared"], TILES * G + t + 1)
            nc.vector.tensor_reduce(ss[:, t, :], sq[:], AX.X, ALU.add).then_inc(S["sq_summed"], 1)

        def rotate(G, half):
            dve.wait_ge(S["qk_copied"], TILES * G + 4 * half + 4)
            x = qk[:, 4 * half:4 * half + 4].rearrange("p t s n -> p (t s) n")
            x1, x2 = x[:, :, 0:ROT], x[:, :, HALF:HALF + ROT]
            tab = [rope[:, i, 4 * half:4 * half + 4].rearrange("p t s n -> p (t s) n") for i in range(4)]
            for dst, src, i in ((prod[:, 0], x2, 1), (prod[:, 1], x1, 3), (x1, x1, 0), (x2, x2, 2)):
                nc.vector.tensor_tensor(dst, src, tab[i], ALU.mult).then_inc(S["rope_prod"], 1)
            dve.wait_ge(S["rope_prod"], 8 * G + 4 * half + 4)
            nc.vector.tensor_tensor(x1, x1, prod[:, 0], ALU.add).then_inc(S["rope_done"], 1)
            nc.vector.tensor_tensor(x2, x2, prod[:, 1], ALU.subtract).then_inc(S["rope_done"], 1)

        def rms(G, half, opening=False):
            v, t = newt[:, 0], newt[:, 1]
            dve.wait_ge(S["sq_summed"], TILES * G + 4 * half + 4)
            if not (opening and half == 0):
                dve.wait_ge(S["rn_made"], 2 * G + half)
            nc.vector.tensor_scalar(v, ss[:, 4 * half:4 * half + 4].rearrange("p t s -> p (t s)"), 1.0 / DK, EPS_RMS,
                                    ALU.mult, ALU.add).then_inc(S["ms_made"], 1)
            dve.wait_ge(S["ms_made"], 2 * G + half + 1)
            nc.vector.tensor_scalar(t.bitcast(I32), v.bitcast(I32), 1, None, ALU.logical_shift_right).then_inc(S["ms_halved"], 1)
            if not opening:
                dve.wait_ge(S["exped"], STEPS * G - 4 + 4 * half)
                dve.wait_ge(S["k_normed"], 2 * G - 1 + half)
            dve.wait_ge(S["ms_halved"], 2 * G + half + 1)
            r = rn[:, 4 * half:4 * half + 4].rearrange("p t s -> p (t s)")
            nc.vector.tensor_scalar(r.bitcast(I32), t.bitcast(I32), -1.0, float(0x5F3759DF), ALU.mult,
                                    ALU.add).then_inc(S["seeded"], 1)

        def low_turned(G, h, pair):
            u = 2 * PAIRS * G + PAIRS * h + pair
            at = slice(2 * pair * P, (2 * pair + 2) * P)
            bank = psX[BANK_OF["turn", h, pair]]
            dve.wait_ge(S["qkT_high"], 2 * u + 2)
            nc.vector.scalar_tensor_tensor(qT[:, h, 1, at], bank[:, 0:2 * P], wq_col[:, 0:1], qT[:, h, 0, at].bitcast(F32),
                                           ALU.mult, ALU.subtract)
            nc.vector.tensor_tensor(kT[:, h, 1, at], bank[:, 2 * P:4 * P], kT[:, h, 0, at].bitcast(F32),
                                    ALU.subtract).then_inc(S["qkT_low"], 1)

        def row_max(G, n):
            t = n % TILES
            dve.wait_ge(S["scored"], STEPS * G + n + 1)
            nc.vector.tensor_reduce(nmax[:, n % 4:n % 4 + 1], psS[:, n % 2, 0:(t + 1) * P], AX.X, ALU.max,
                                    negate=True).then_inc(S["max_made"], 1)
            dve.wait_ge(S["max_made"], STEPS * G + n + 1)
            if n == 0:
                dve.wait_ge(S["rn_made"], 2 * G + 1)
            if n == 4:
                dve.wait_ge(S["rn_made"], 2 * G + 2)
            nc.vector.tensor_tensor(bias[:, n % 4:n % 4 + 1], nmax[:, n % 4:n % 4 + 1],
                                    rn[:, t, n // TILES:n // TILES + 1], ALU.mult).then_inc(S["bias_made"], 1)

        def invert(G, n):
            dve.wait_ge(S["exped"], STEPS * G + n + 1)
            nc.vector.reciprocal(rinv[:, n % 4:n % 4 + 1], rsum[:, n % 4:n % 4 + 1]).then_inc(S["rinv_made"], 1)

        def low_values(G, u):
            h, pair = u // PAIRS, u % PAIRS
            at = slice(2 * pair * P, (2 * pair + 2) * P)
            dve.wait_ge(S["attn_high"], 2 * PAIRS * G + u + 1)
            nc.vector.tensor_tensor(attnT[:, 1, h, at], psX[BANK_OF["values", u]][:, 0:2 * P], attnT[:, 0, h, at].bitcast(F32),
                                    ALU.subtract).then_inc(S["attn_low"], 1)

        def low_probs(G, n):
            t, u = n % TILES, n // 2
            for c in range(t // 4 + 1):
                dve.wait_ge(S["pT_high"], NCH * G + CHUNK[n] + c + 1)
                k = min(4, t + 1 - 4 * c)
                at = (slice(None), slice(4 * c, 4 * c + k), slice((n % 2) * P, (n % 2 + 1) * P))
                nc.vector.tensor_tensor(pT[u % 2][:, 1][at], psT[c][:, 0:k * P].rearrange("p (j q) -> p j q", q=P),
                                        pT[u % 2][:, 0][at].bitcast(F32), ALU.subtract).then_inc(S["pT_low"], 1)

        def add_rows(G, t, bank):
            dve.wait_ge(S["rows_made"], TILES * G + t + 1)
            nc.vector.tensor_tensor(acc[:, t, :], bank[:], acc[:, t, :], ALU.add).then_inc(S["rows_added"], 1)

        def body(G, first, last):
            for n in range(STEPS):
                if n + 2 < STEPS:
                    row_max(G, n + 2)
                elif not last:
                    row_max(G + 1, n + 2 - STEPS)
                if n % 2 and not (first and n == 1):
                    low_values(G, n // 2 - 1) if n > 1 else low_values(G - 1, 2 * PAIRS - 1)
                for t in OUT_AT.get(n, []) if not first else []:
                    add_rows(G - 1, t, psX[BANK_OF["rows", t]])
                for t in PROJ_AT.get(n, []) if not last else []:
                    sum_squares(G + 1, t)
                if n in TURN_AT:
                    ahead, h, pair = TURN_AT[n]
                    if not (ahead and last):
                        low_turned(G + ahead, h, pair)
                low_probs(G, n)
                if n + 2 < STEPS:
                    invert(G, n + 2)
                elif not last:
                    invert(G + 1, n + 2 - STEPS)
                if not last:
                    for at, half in ((9, 0), (13, 1)):
                        if n == at:
                            rms(G + 1, half)
                            rotate(G + 1, half)

        for t in range(TILES):
            dve.wait_ge(x_in[t // 2], 16 * b + 16)
            nc.vector.bn_stats(stats[:, t, :], acc[:, t, :]).then_inc(S["ln_stats"], 1)
        for t in range(TILES):
            hold(dve, S["ln_stats"], TILES * b + t + 1)
            nc.vector.bn_aggr(mv[:, t, :], stats[:, t, :]).then_inc(S["ln_mean"], 1)
        dve.wait_ge(S["ln_mean"], TILES * b + TILES)
        nc.vector.tensor_scalar(newt[:, 0, 0:TILES], mv[:, :, 1], EPS_LN, None, ALU.add).then_inc(S["ln_var"], 1)
        dve.wait_ge(S["ln_var"], b + 1)
        rsqrt(dve, S["ln_rsqrt"], RSQRT_OPS * b, newt[:, 0, 0:TILES], rstd[:], newt[:, 1, 0:TILES])

        def normed_rows(t):
            if t >= 2:
                dve.wait_ge(S["xn_turned"], TILES * b + t - 1)
            nc.vector.tensor_scalar(xn[t % 2][:, 0:DIM], acc[:, t, :], mv[:, t, 0:1], rstd[:, t:t + 1],
                                    ALU.subtract, ALU.mult).then_inc(S["xn_made"], 1)

        normed_rows(0)
        for t in range(TILES):
            if t + 1 < TILES:
                normed_rows(t + 1)
            dve.wait_ge(S["xnT_high"], TILES * b + t + 1)
            at = (slice(None), slice(None), slice(t * P, (t + 1) * P))
            nc.vector.tensor_tensor(xnT[:, 1][at], psT[t % 2][:].rearrange("p (c q) -> p c q", q=P),
                                    xnT[:, 0][at].bitcast(F32), ALU.subtract).then_inc(S["xnT_low"], 1)
        for q in range(2):
            dve.wait_ge(S["latT_high"], 2 * b + q + 1)
            at = slice(q * BANK, (q + 1) * BANK)
            nc.vector.tensor_tensor(latT[:, 1, at], psX[q][:], latT[:, 0, at].bitcast(F32),
                                    ALU.subtract).then_inc(S["latT_low"], 1)
        for q in range(2):
            dve.wait_ge(S["lat_turned"], 4 * b + 2 * q + 2)
            nc.vector.tensor_copy(lat[:, 1, 4 * q:4 * q + 4, :],
                                  psT[1][:].rearrange("p (j n) -> p j n", n=P)).then_inc(S["lat_low"], 1)
        G0 = b * GROUPS
        for half in range(2):
            for t in range(4):
                sum_squares(G0, 4 * half + t)
            rms(G0, half, opening=True)
            rotate(G0, half)
        low_turned(G0, 0, 0)
        low_turned(G0, 0, 1)
        row_max(G0, 0)
        row_max(G0, 1)
        invert(G0, 0)
        invert(G0, 1)
        groups(dve, body)
        low_values(G0 + (GROUPS - 1), 2 * PAIRS - 1)
        for t in range(TILES):
            add_rows(G0 + (GROUPS - 1), t, psX[(t + 1) % 2])

    @block.tensor
    def _(pe):
        def parts(x, *at):
            return x[(slice(None), 0) + at], x[(slice(None), 1) + at]

        def project(G, t, bank, free):
            if t == 0:
                pe.wait_ge(S["wqk_in"], 16 * G + 16)
            if free:
                pe.wait_ge(*free)
            at = slice(t * P, (t + 1) * P)
            for c in range(CHUNKS):
                mm3(bank[:, 0:GW], parts(xnT, c, at), parts(wqk, c), c == 0, c == CHUNKS - 1)
            mm3(bank[:, GW:2 * GW], parts(latT, at), parts(wqk, CHUNKS), True, True).then_inc(S["projected"], 1)

        def turn(G, h, pair, free):
            if pair in (0, 2):
                pe.wait_ge(S["rope_done"], 4 * G + 2 * (pair // 2) + 2)
                pe.wait_ge(S["k_normed"], 2 * G + pair // 2 + 1)
            pe.wait_ge(*free)
            for i, (slot, j) in enumerate(((h, 0), (h, 1), (PAIR + h, 0), (PAIR + h, 1))):
                last = nc.tensor.transpose(psX[BANK_OF["turn", h, pair]][:, i * P:(i + 1) * P], qk[:, 2 * pair + j, slot, :], ident[:])
            last.then_inc(S["qk_turned"], 1)

        def score(G, n, opening=False):
            h, t = n // TILES, n % TILES
            if t % 2 == 0:
                pe.wait_ge(S["qkT_low"], 2 * PAIRS * G + PAIRS * h + t // 2 + 1)
            if not opening:
                pe.wait_ge(S["exped"], STEPS * G + n - 1)
            q = parts(qT[:, h], slice(t * P, (t + 1) * P))
            for first in range(0, t + 1, 4):
                at = slice(first * P, min(first + 4, t + 1) * P)
                diagonal = first + 4 > t
                last = mm3(psS[:, n % 2, at], q, parts(kT[:, h], at), True, not diagonal)
                if diagonal:
                    last = nc.tensor.matmul(psS[:, n % 2, t * P:(t + 1) * P], ident_b[:], causal[:], start=False, stop=True)
            last.then_inc(S["scored"], 1)

        def turn_probs(G, n, opening):
            t = n % TILES
            pe.wait_ge(S["normed"], STEPS * G + n + 1)
            for c in range(t // 4 + 1):
                if c == 0:
                    before = CHUNK[n - 1] + 1 if n else CHUNK[STEPS - 1] + 1 - NCH
                else:
                    before = CHUNK[n - 1] + 2 if t > 4 else (CHUNK[7] + 2 if n >= TILES else CHUNK[15] + 2 - NCH)
                if not (opening and before < 0 or opening and n == 0):
                    pe.wait_ge(S["pT_low"], NCH * G + before)
                for j in range(4 * c, min(4 * c + 4, t + 1)):
                    last = nc.tensor.transpose(psT[c][:, (j - 4 * c) * P:(j - 4 * c + 1) * P],
                                               probs[n % 4][:, j * P:(j + 1) * P], ident[:])
                last.then_inc(S["p_turned"], 1)

        def values(G, u, free):
            pair = u % PAIRS
            pe.wait_ge(S["pT_low"], NCH * G + CHUNK[2 * u + 2])
            pe.wait_ge(*free)
            for j in range(2 * pair + 2):
                at = slice(0, 2 * P) if j <= 2 * pair else slice(P, 2 * P)
                last = mm3(psX[BANK_OF["values", u]][:, at], parts(lat, j), parts(pT[u % 2], j, at), j == 0, j == 2 * pair + 1)
            last.then_inc(S["valued"], 1)

        def rows(G, t, bank, free):
            if t == 0:
                pe.wait_ge(S["wvo_in"], 16 * G + 16)
            if free[0] is not S["attn_low"]:
                pe.wait_ge(S["attn_low"], 2 * PAIRS * G + PAIRS + t // 2 + 1)
            pe.wait_ge(*free)
            for h in range(PAIR):
                last = mm3(bank[:], parts(attnT, h, slice(t * P, (t + 1) * P)), parts(wvo, h), h == 0, h == PAIR - 1)
            last.then_inc(S["rows_made"], 1)

        free = [None, None]

        def body(G, first, last):
            free[BANK_OF["turn", 0, 1]] = (S["qkT_low"], 2 * PAIRS * G + 2)
            free[1 - BANK_OF["turn", 0, 1]] = (S["qkT_low"], 2 * PAIRS * G + 1) if first else (S["attn_low"], 2 * PAIRS * G - 1)
            for n in range(STEPS):
                if n + 2 < STEPS:
                    score(G, n + 2)
                elif not last:
                    score(G + 1, n + 2 - STEPS)
                if n % 2 and not (first and n == 1):
                    g, u = (G, n // 2 - 1) if n > 1 else (G - 1, 2 * PAIRS - 1)
                    k = BANK_OF["values", u]
                    values(g, u, free[k])
                    free[k] = (S["attn_low"], 2 * PAIRS * g + u + 1)
                for t in OUT_AT.get(n, []) if not first else []:
                    k = BANK_OF["rows", t]
                    rows(G - 1, t, psX[k], free[k])
                    free[k] = (S["rows_added"], TILES * (G - 1) + t + 1)
                for t in PROJ_AT.get(n, []) if not last else []:
                    k = BANK_OF["project", t]
                    project(G + 1, t, psX[k], free[k])
                    free[k] = (S["qk_copied"], TILES * (G + 1) + t + 1)
                if n in TURN_AT:
                    ahead, h, pair = TURN_AT[n]
                    if not (ahead and last):
                        k = BANK_OF["turn", h, pair]
                        turn(G + ahead, h, pair, free[k])
                        free[k] = (S["qkT_low"], 2 * PAIRS * (G + ahead) + PAIRS * h + pair + 1)
                turn_probs(G, n, first)

        for t in range(TILES):
            pe.wait_ge(S["xn_made"], TILES * b + t + 1)
            if t >= 2:
                pe.wait_ge(S["xnT_low"], TILES * b + t - 1)
            for c in range(CHUNKS):
                last = nc.tensor.transpose(psT[t % 2][:, c * P:(c + 1) * P], xn[t % 2][:, c * P:(c + 1) * P], ident[:])
            last.then_inc(S["xn_turned"], 1)
        for q in range(2):
            pe.wait_ge(S["xnT_low"], TILES * b + 4 * q + 4)
            for c in range(CHUNKS):
                last = mm3(psX[q][:], parts(kvd, c), parts(xnT, c, slice(q * BANK, (q + 1) * BANK)), c == 0, c == CHUNKS - 1)
            last.then_inc(S["lat_made"], 1)
        for q in range(2):
            pe.wait_ge(S["latT_low"], 2 * b + q + 1)
            for part in range(2):
                if q:
                    pe.wait_ge(S["lat_high"] if part == 0 else S["lat_low"], 2 * b + 1)
                for j in range(4):
                    at = slice((4 * q + j) * P, (4 * q + j + 1) * P)
                    last = nc.tensor.transpose(psT[part][:, j * P:(j + 1) * P], latT[:, part, at].bitcast(F32), ident[:])
                last.then_inc(S["lat_turned"], 1)
        G0 = b * GROUPS
        for t in range(TILES):
            project(G0, t, psX[t % 2], (S["qk_copied"], TILES * G0 + t - 1) if t >= 2 else (S["latT_low"], 2 * b + t + 1))
        turn(G0, 0, 0, (S["qk_copied"], TILES * G0 + TILES))
        turn(G0, 0, 1, (S["qk_copied"], TILES * G0 + TILES))
        score(G0, 0, opening=True)
        score(G0, 1, opening=True)
        groups(pe, body)
        G = G0 + (GROUPS - 1)
        k = BANK_OF["values", 2 * PAIRS - 1]
        values(G, 2 * PAIRS - 1, free[k])
        free[k] = (S["attn_low"], 2 * PAIRS * G + 2 * PAIRS)
        for t in range(TILES):
            k = (t + 1) % 2
            rows(G, t, psX[k], free[k])
            free[k] = (S["rows_added"], TILES * G + t + 1)


def split_ffn(nc, a, sem, sb, m):
    ffn_in, ffn_high, ffn_low, ffn_out = sem("ffn_in"), sem("ffn_high"), sem("ffn_low"), sem("ffn_out")
    with ExitStack() as st:
        gu_raw = sb(st, "gu_raw", [P, CHUNKS, 2, INNER])
        dn_raw = sb(st, "dn_raw", [P, 2, DIM])
        rt_raw = sb(st, "rt_raw", [P, CHUNKS, EXPERTS])
        rt_rows = sb(st, "rt_rows", [EXPERTS, DIM])
        gu = sb(st, "gu_parts", [P, 2, CHUNKS, GU], F32R)
        dn = sb(st, "dn_parts", [P, 2, 2, DIM], F32R)
        rt = sb(st, "rt_parts", [P, 2, CHUNKS, EXPERTS], F32R)
        zero = sb(st, "zero", [P, DIM])
        table = sb(st, "table", [P, SLOTS // P, 2], I32)
        padded, turned, turned_out, zeroed, empty = sem("padded"), sem("rt_turned"), sem("rt_turned_copied"), sem("zeroed"), sem("table_empty")
        block = st.enter_context(nc.Block())

        @block.sync
        def _(sp):
            sp.dma_start(rt_rows[:], a["router"]).then_inc(sem("rt_in"), 16)
            sp.wait_ge(padded, 2)
            sp.dma_start(gu_raw[:, :, 0, :], a["sh_gate"].rearrange("(c p) n -> p c n", p=P)).then_inc(ffn_in, 16)
            sp.dma_start(gu_raw[:, :, 1, :], a["sh_up"].rearrange("(c p) n -> p c n", p=P)).then_inc(ffn_in, 16)
            sp.dma_start(dn_raw[:, 0, :], a["sh_down"][0:P, :]).then_inc(ffn_in, 16)
            sp.dma_start(dn_raw[0:TAIL, 1, :], a["sh_down"][P:INNER, :]).then_inc(ffn_in, 16)
            sp.wait_ge(zeroed, 1)
            for i in range(CHALF):
                sp.dma_start(m["xn_rows"][TOKENS + i * P:TOKENS + (i + 1) * P, :], zero[:]).then_inc(ffn_out, 16)
                sp.dma_start(m["sum_rows"][TOKENS + i * P:TOKENS + (i + 1) * P, :], zero[:]).then_inc(ffn_out, 16)
            sp.wait_ge(empty, 2)
            sp.dma_start(m["slot_table"].rearrange("(p n) w -> p n w", p=P), table[:]).then_inc(ffn_out, 16)
            sp.wait_ge(ffn_low, 4)
            sp.dma_start(m["gu_split"], gu[:].bitcast(F32)).then_inc(ffn_out, 16)
            sp.dma_start(m["dn_split"], dn[:].bitcast(F32)).then_inc(ffn_out, 16)
            sp.dma_start(m["rt_split"], rt[:].bitcast(F32)).then_inc(ffn_out, 16)
            sp.wait_ge(ffn_out, 16 * (2 * CHALF + 4))

        @block.gpsimd
        def _(pool):
            nc.gpsimd.memset(gu[:].bitcast(F32), 0.0).then_inc(padded, 1)
            nc.gpsimd.memset(dn_raw[:], 0.0).then_inc(padded, 1)
            nc.gpsimd.memset(zero[:], 0.0).then_inc(zeroed, 1)
            nc.gpsimd.iota(table[:, :, 0].rearrange("p (e h) -> p e h", h=CHALF), pattern=[[0, EXPERTS], [P, CHALF]],
                           base=TOKENS, channel_multiplier=1).then_inc(empty, 1)
            nc.gpsimd.memset(table[:, :, 1], 0).then_inc(empty, 1)

        @block.tensor
        def _(pe):
            pe.wait_ge(sem("rt_in"), 16)
            for c in range(CHUNKS):
                last = nc.tensor.transpose(m["banks"][0][:, c * EXPERTS:(c + 1) * EXPERTS], rt_rows[:, c * P:(c + 1) * P],
                                           m["ident"][0:EXPERTS, 0:EXPERTS])
            last.then_inc(turned, 1)

        @block.scalar
        def _(act):
            act.wait_ge(turned, 1)
            nc.scalar.activation(rt_raw[:].rearrange("p c n -> p (c n)"), m["banks"][0][:, 0:CHUNKS * EXPERTS],
                                 ACT.Copy).then_inc(turned_out, 1)
            act.wait_ge(turned_out, 1)
            nc.scalar.activation(rt[:, 0], rt_raw[:], ACT.Copy).then_inc(ffn_high, 1)
            act.wait_ge(ffn_in, 64)
            act.wait_ge(padded, 2)
            for dst, src in gu_views(gu[:, 0], gu_raw):
                nc.scalar.activation(dst, src, ACT.Copy).then_inc(ffn_high, 1)
            nc.scalar.activation(dn[:, 0], dn_raw[:], ACT.Copy).then_inc(ffn_high, 1)

        @block.vector
        def _(dve):
            dve.wait_ge(ffn_high, 1)
            nc.vector.tensor_tensor(rt[:, 1], rt_raw[:], rt[:, 0].bitcast(F32), ALU.subtract).then_inc(ffn_low, 1)
            for i, ((low, raw), (high, _)) in enumerate(zip(gu_views(gu[:, 1], gu_raw), gu_views(gu[:, 0], gu_raw))):
                dve.wait_ge(ffn_high, i + 2)
                nc.vector.tensor_tensor(low, raw, high.bitcast(F32), ALU.subtract).then_inc(ffn_low, 1)
            dve.wait_ge(ffn_high, 4)
            nc.vector.tensor_tensor(dn[:, 1], dn_raw[:], dn[:, 0].bitcast(F32), ALU.subtract).then_inc(ffn_low, 1)


def route(nc, a, b, sem, sb, st, mm3, rsqrt, RSQRT_OPS, m):
    ident, acc, psT, psX, psS = m["ident"], m["acc"], m["psT"], m["psX"], m["psS"]
    hold = holder(sem)
    W = QUAD * P
    QUADS = TILES // QUAD
    bank = [psS[:, i // 2, (i % 2) * BANK:(i % 2 + 1) * BANK] for i in range(4)]
    gu = sb(st, "gu_sh", [P, 2, CHUNKS, GU], F32R)
    dn = sb(st, "dn_sh", [P, 2, 2, DIM], F32R)
    rt = sb(st, "rt_sh", [P, 2, CHUNKS, EXPERTS], F32R)
    stats = sb(st, "stats2", [P, QUAD, 6])
    mv = sb(st, "mv2", [P, QUAD, 2])
    var = sb(st, "var2", [P, QUAD])
    rstd = sb(st, "rstd2", [P, QUAD])
    temp = sb(st, "temp2", [P, QUAD])
    xn = sb(st, "xn2", [P, QUAD, DIM])
    xnT = sb(st, "xnT2", [P, 2, CHUNKS, W], F32R)
    gate = sb(st, "gate2", [P, 2, W])
    inner = sb(st, "inner2", [P, 2, W])
    hT = sb(st, "hT2", [P, 2, 2, W], F32R)
    base = sb(st, "base2", [P, QUAD, DIM])
    score = sb(st, "score2", [P, QUAD, EXPERTS])
    biased = sb(st, "biased2", [P, QUAD, EXPERTS])
    hi4, lo4 = sb(st, "hi4", [P, QUAD * EGROUPS, 4]), sb(st, "lo4", [P, QUAD * EGROUPS, 4])
    hi2, lo2, mid2, low2 = [sb(st, n, [P, QUAD * EGROUPS, 2]) for n in ("hi2", "lo2", "mid2", "low2")]
    hi1, lo1, mid1, low1 = [sb(st, n, [P, QUAD * EGROUPS, 1]) for n in ("hi1", "lo1", "mid1", "low1")]
    gsum = sb(st, "gsum", [P, QUAD, EGROUPS])
    above = sb(st, "above", [P, QUAD, EGROUPS, EGROUPS])
    equal = sb(st, "equal", [P, QUAD, EGROUPS, EGROUPS])
    rank = sb(st, "rank", [P, QUAD, EGROUPS])
    keep = sb(st, "keep", [P, QUAD, EGROUPS])
    masked = sb(st, "masked", [P, QUAD, EXPERTS])
    replaced = sb(st, "replaced", [P, QUAD, EXPERTS])
    chosen = sb(st, "chosen", [P, QUAD, EXPERTS], BF16)
    chosen_sum = sb(st, "chosen_sum", [P, EXPERTS], BF16)
    best = sb(st, "best", [P, QUAD, TOPK])
    expert = sb(st, "expert", [P, QUAD, TOPK], U32)
    half = sb(st, "half", [P, QUAD, EXPERTS])
    row = sb(st, "row", [P, QUAD, EXPERTS])
    onehot = sb(st, "onehot", [P, 2, TOPK, EXPERTS])
    prod_row = sb(st, "prod_row", [P, 2, TOPK, EXPERTS])
    prod_score = sb(st, "prod_score", [P, 2, TOPK, EXPERTS])
    row_f = sb(st, "row_f", [P, QUAD, TOPK])
    score_k = sb(st, "score_k", [P, QUAD, TOPK])
    score_sum = sb(st, "score_sum", [P, QUAD])
    table_row = m["table_row"]
    entry = m["entry"]
    seen, token, lower, before, ones, number, number2, bias_row = (
        m[k] for k in ("seen", "token", "lower", "before", "ones", "number", "number2", "bias_row"))
    names = ("ffn_w_in", "mean2", "var2", "rsqrt2", "xn2_made", "xn2_out", "xn2_turned", "xnT2_high", "xnT2_low",
             "logits", "scores_made", "chain", "chosen_made", "seen_made", "gated", "silu_made", "inner_made", "inner_high",
             "inner_low", "placed", "rows_ready", "onehot_made", "prods_made", "entries_made", "scattered",
             "down_made", "base_made", "base_out", "stats2_made")
    S = {n: sem("r_" + n) for n in names}
    block = st.enter_context(nc.Block())
    CHAIN = 27

    def quads(body):
        for q in range(QUADS):
            body(q, b * QUADS + q)

    @block.sync
    def _(sp):
        sp.dma_start(gu[:].bitcast(F32), m["gu_split"]).then_inc(S["ffn_w_in"], 16)
        sp.dma_start(dn[:].bitcast(F32), m["dn_split"]).then_inc(S["ffn_w_in"], 16)
        sp.dma_start(rt[:].bitcast(F32), m["rt_split"]).then_inc(S["ffn_w_in"], 16)

        def body(q, Q):
            rows = bass.ds(Q * W, W)
            hold(sp, S["xn2_made"], Q * QUAD + QUAD)
            sp.dma_start(m["xn_rows"][rows, :].rearrange("(t p) d -> p t d", p=P), xn[:]).then_inc(S["xn2_out"], 16)
            hold(sp, S["base_made"], Q * QUAD + QUAD)
            sp.dma_start(m["sum_rows"][rows, :].rearrange("(t p) d -> p t d", p=P), base[:]).then_inc(S["base_out"], 16)

        quads(body)
        hold(sp, S["xn2_out"], (b + 1) * (16 * QUADS))
        hold(sp, S["base_out"], (b + 1) * (16 * QUADS))

    @block.gpsimd
    def _(pool):
        def body(q, Q):
            for t in range(QUAD):
                k = t % 2
                hold(pool, S["onehot_made"], Q * QUAD + t + 1)
                nc.gpsimd.tensor_tensor(prod_row[:, k], onehot[:, k], row[:, t].unsqueeze(1).to_broadcast([P, TOPK, EXPERTS]),
                                        ALU.mult).then_inc(S["prods_made"], 1)
                nc.gpsimd.tensor_tensor(prod_score[:, k], onehot[:, k], score[:, t].unsqueeze(1).to_broadcast([P, TOPK, EXPERTS]),
                                        ALU.mult).then_inc(S["prods_made"], 1)
            hold(pool, S["entries_made"], Q * 2 + 2)
            for t in range(QUAD):
                for k in range(TOPK):
                    nc.gpsimd.indirect_dma_start(
                        m["slot_table"], bass.IndirectOffsetOnAxis(table_row[:, t, k:k + 1], 0),
                        entry[:, t, k, :], None, bounds_check=SLOTS - 1, oob_is_err=False).then_inc(S["scattered"], 16)
            hold(pool, S["scattered"], (Q + 1) * (16 * QUAD * TOPK))

        quads(body)

    @block.scalar
    def _(act):
        def body(q, Q):
            for t in range(QUAD):
                act.wait_ge(S["xn2_turned"], Q * QUAD + t + 1)
                nc.scalar.activation(xnT[:, 0, :, t * P:(t + 1) * P], bank[t].rearrange("p (c n) -> p c n", n=P),
                                     ACT.Copy).then_inc(S["xnT2_high"], 1)
            act.wait_ge(S["logits"], Q + 1)
            nc.scalar.activation(score[:].rearrange("p t n -> p (t n)"), psT[0][:, 0:QUAD * EXPERTS],
                                 ACT.Sigmoid).then_inc(S["scores_made"], 1)
            act.wait_ge(S["gated"], Q * 3 + 3)
            nc.scalar.activation(gate[:, 0], psX[0][:], ACT.Silu).then_inc(S["silu_made"], 1)
            nc.scalar.activation(gate[0:TAIL, 1], bank[0][0:TAIL], ACT.Silu).then_inc(S["silu_made"], 1)
            act.wait_ge(S["inner_made"], Q * 2 + 2)
            nc.scalar.activation(hT[:, 0, 0], inner[:, 0], ACT.Copy).then_inc(S["inner_high"], 1)
            nc.scalar.activation(hT[0:TAIL, 0, 1], inner[0:TAIL, 1], ACT.Copy).then_inc(S["inner_high"], 1)

        quads(body)

    @block.vector
    def _(dve):
        def body(q, Q):
            link = [0]

            def after(ins):
                link[0] += 1
                ins.then_inc(S["chain"], 1)
                hold(dve, S["chain"], Q * CHAIN + link[0])

            for t in range(QUAD):
                last = nc.vector.bn_stats(stats[:, t, :], acc[:, q * QUAD + t, :])
            after(last)
            for t in range(QUAD):
                last = nc.vector.bn_aggr(mv[:, t, :], stats[:, t, :])
            after(last)
            after(nc.vector.tensor_scalar(var[:], mv[:, :, 1], EPS_LN, None, ALU.add))
            rsqrt(dve, S["rsqrt2"], RSQRT_OPS * Q, var[:], rstd[:], temp[:])
            if q:
                dve.wait_ge(S["xn2_out"], 16 * Q)
            for t in range(QUAD):
                nc.vector.tensor_scalar(xn[:, t], acc[:, q * QUAD + t, :], mv[:, t, 0:1], rstd[:, t:t + 1],
                                        ALU.subtract, ALU.mult).then_inc(S["xn2_made"], 1)
            for t in range(QUAD):
                dve.wait_ge(S["xnT2_high"], Q * QUAD + t + 1)
                at = (slice(None), slice(None), slice(t * P, (t + 1) * P))
                nc.vector.tensor_tensor(xnT[:, 1][at], bank[t].rearrange("p (c n) -> p c n", n=P), xnT[:, 0][at].bitcast(F32),
                                        ALU.subtract).then_inc(S["xnT2_low"], 1)
            dve.wait_ge(S["scores_made"], Q + 1)
            after(nc.vector.tensor_tensor(biased[:], score[:], bias_row[:].unsqueeze(1).to_broadcast([P, QUAD, EXPERTS]), ALU.add))
            x = biased[:].rearrange("p t (g n) -> p (t g) n", n=EG)
            nc.vector.tensor_tensor(hi4[:], x[:, :, 0:4], x[:, :, 4:8], ALU.max)
            after(nc.vector.tensor_tensor(lo4[:], x[:, :, 0:4], x[:, :, 4:8], ALU.min))
            for h, l, n, h_, l_, mid, low in ((hi4, lo4, 2, hi2, lo2, mid2, low2), (hi2, lo2, 1, hi1, lo1, mid1, low1)):
                nc.vector.tensor_tensor(h_[:], h[:, :, 0:n], h[:, :, n:2 * n], ALU.max)
                nc.vector.tensor_tensor(mid[:], h[:, :, 0:n], h[:, :, n:2 * n], ALU.min)
                after(nc.vector.tensor_tensor(low[:], l[:, :, 0:n], l[:, :, n:2 * n], ALU.max))
                after(nc.vector.tensor_tensor(l_[:], mid[:], low[:], ALU.max))
            after(nc.vector.tensor_tensor(gsum[:].rearrange("p t g -> p (t g)"), hi1[:, :, 0], lo1[:, :, 0], ALU.add))
            full = [P, QUAD, EGROUPS, EGROUPS]
            other, own = gsum[:].unsqueeze(2).to_broadcast(full), gsum[:].unsqueeze(3).to_broadcast(full)
            nc.vector.tensor_tensor(above[:], other, own, ALU.is_gt)
            after(nc.vector.tensor_tensor(equal[:], other, own, ALU.is_equal))
            after(nc.vector.tensor_tensor(equal[:], equal[:], lower[:].unsqueeze(1).to_broadcast(full), ALU.mult))
            after(nc.vector.tensor_tensor(above[:], above[:], equal[:], ALU.add))
            after(nc.vector.tensor_reduce(rank[:], above[:], AX.X, ALU.add))
            after(nc.vector.tensor_scalar(keep[:], rank[:], float(TOPG), None, ALU.is_lt))
            after(nc.vector.tensor_tensor(masked[:].rearrange("p t (g n) -> p (t g) n", n=EG), x,
                                          keep[:].rearrange("p t g -> p (t g)").unsqueeze(2).to_broadcast([P, QUAD * EGROUPS, EG]), ALU.mult))
            after(nc.vector.tensor_scalar(masked[:], masked[:], 0.0, None, ALU.add))
            for t in range(QUAD):
                last = nc.vector.max(best[:, t], masked[:, t])
            after(last)
            for t in range(QUAD):
                nc.vector.max_index(expert[:, t], best[:, t], masked[:, t])
                last = nc.vector.match_replace(replaced[:, t], best[:, t], masked[:, t], MASKED)
            after(last)
            nc.vector.tensor_tensor(chosen[:], replaced[:], masked[:], ALU.not_equal).then_inc(S["chosen_made"], 1)
            dve.wait_ge(S["silu_made"], Q * 2 + 2)
            nc.vector.tensor_tensor(inner[:, 0], gate[:, 0], psX[1][:], ALU.mult).then_inc(S["inner_made"], 1)
            nc.vector.tensor_tensor(inner[0:TAIL, 1], gate[0:TAIL, 1], bank[0][64:64 + TAIL], ALU.mult).then_inc(S["inner_made"], 1)
            dve.wait_ge(S["inner_high"], Q * 2 + 2)
            nc.vector.tensor_tensor(hT[:, 1, 0], inner[:, 0], hT[:, 0, 0].bitcast(F32), ALU.subtract).then_inc(S["inner_low"], 1)
            nc.vector.tensor_tensor(hT[0:TAIL, 1, 1], inner[0:TAIL, 1], hT[0:TAIL, 0, 1].bitcast(F32), ALU.subtract).then_inc(S["inner_low"], 1)
            dve.wait_ge(S["placed"], Q + 1)
            slot = psT[1][:, 0:QUAD * EXPERTS].rearrange("p (t n) -> p t n", n=EXPERTS)
            after(nc.vector.tensor_scalar(half[:], slot, float(P), float(P * P - 1), ALU.is_ge, ALU.mult))
            after(nc.vector.scalar_tensor_tensor(row[:], slot, float(P), half[:], ALU.mult, ALU.subtract))
            after(nc.vector.tensor_tensor(row[:], row[:], number2[:].unsqueeze(1).to_broadcast([P, QUAD, EXPERTS]), ALU.add))
            nc.vector.tensor_reduce(half[:, 0], chosen[:].rearrange("p t n -> p n t"), AX.X, ALU.add).then_inc(S["seen_made"], 1)
            hold(dve, S["seen_made"], Q * 2 + 1)
            nc.vector.tensor_tensor(seen[:], seen[:], half[:, 0], ALU.add).then_inc(S["seen_made"], 1)
            full = [P, TOPK, EXPERTS]

            def pick(t):
                hold(dve, S["prods_made"], Q * (2 * QUAD) + 2 * t + 2)
                nc.vector.tensor_reduce(row_f[:, t], prod_row[:, t % 2], AX.X, ALU.add)
                return nc.vector.tensor_reduce(score_k[:, t], prod_score[:, t % 2], AX.X, ALU.add)

            for t in range(QUAD):
                nc.vector.tensor_tensor(onehot[:, t % 2], number[:].unsqueeze(1).to_broadcast(full),
                                        expert[:, t].unsqueeze(2).to_broadcast(full), ALU.is_equal).then_inc(S["onehot_made"], 1)
                if t:
                    pick(t - 1)
            after(pick(QUAD - 1))
            after(nc.vector.tensor_reduce(score_sum[:], score_k[:], AX.X, ALU.add))
            after(nc.vector.tensor_scalar(score_sum[:], score_sum[:], 1e-20, None, ALU.add))
            after(nc.vector.reciprocal(score_sum[:], score_sum[:]))
            after(nc.vector.tensor_scalar(score_sum[:], score_sum[:], SCALE_ROUTE, None, ALU.mult))
            if q:
                dve.wait_ge(S["scattered"], Q * (16 * QUAD * TOPK))
            nc.vector.tensor_tensor(entry[:, :, :, 1].bitcast(F32), score_k[:], score_sum[:].unsqueeze(2).to_broadcast([P, QUAD, TOPK]), ALU.mult)
            nc.vector.tensor_copy(entry[:, :, :, 0], token[:].unsqueeze(2).to_broadcast([P, QUAD, TOPK])).then_inc(S["entries_made"], 1)
            nc.vector.tensor_copy(table_row[:], row_f[:]).then_inc(S["entries_made"], 1)
            hold(dve, S["entries_made"], Q * 2 + 1)
            nc.vector.tensor_scalar(token[:], token[:], float(W), None, ALU.add)
            if q:
                dve.wait_ge(S["base_out"], 16 * Q)
            for t in range(QUAD):
                dve.wait_ge(S["down_made"], Q * QUAD + t + 1)
                nc.vector.tensor_tensor(base[:, t], bank[1 + t % 2], acc[:, q * QUAD + t, :], ALU.add).then_inc(S["base_made"], 1)
            assert link[0] == CHAIN, link[0]

        quads(body)

    @block.tensor
    def _(pe):
        def parts(x, *at):
            return x[(slice(None), 0) + at], x[(slice(None), 1) + at]

        def body(q, Q):
            for t in range(QUAD):
                pe.wait_ge(S["xn2_made"], Q * QUAD + t + 1)
                if q and t in (1, 2):
                    pe.wait_ge(S["base_made"], Q * QUAD)
                for c in range(CHUNKS):
                    last = nc.tensor.transpose(bank[t][:, c * P:(c + 1) * P], xn[:, t, c * P:(c + 1) * P], ident[:])
                last.then_inc(S["xn2_turned"], 1)
            pe.wait_ge(S["ffn_w_in"], b * 48 + 48)
            for t in range(QUAD):
                pe.wait_ge(S["xnT2_low"], Q * QUAD + t + 1)
                for c in range(CHUNKS):
                    last = mm3(psT[0][:, t * EXPERTS:(t + 1) * EXPERTS], parts(xnT, c, slice(t * P, (t + 1) * P)), parts(rt, c),
                               c == 0, c == CHUNKS - 1)
            last.then_inc(S["logits"], 1)
            inner_tiles = [(psX[0][:], slice(0, P)), (psX[1][:], slice(P, 2 * P)), (bank[0], slice(2 * P, GU))]
            for dst, at in inner_tiles:
                for c in range(CHUNKS):
                    last = mm3(dst, parts(gu, c, at), parts(xnT, c), c == 0, c == CHUNKS - 1)
                last.then_inc(S["gated"], 1)
            pe.wait_ge(S["chosen_made"], Q + 1)
            if q:
                pe.wait_ge(S["seen_made"], Q * 2)
            for t in range(QUAD):
                dst = psT[1][:, t * EXPERTS:(t + 1) * EXPERTS]
                nc.tensor.matmul(dst, before[:], chosen[:, t], start=True, stop=False)
                for earlier in range(t):
                    nc.tensor.matmul(dst, ones[:], chosen[:, earlier], start=False, stop=False)
                last = nc.tensor.matmul(dst, ones[:], seen[:], start=False, stop=True)
            last.then_inc(S["placed"], 1)
            pe.wait_ge(S["inner_low"], Q * 2 + 2)
            for t in range(QUAD):
                if t >= 2:
                    pe.wait_ge(S["base_made"], Q * QUAD + t - 1)
                at = slice(t * P, (t + 1) * P)
                mm3(bank[1 + t % 2], parts(hT, 0, at), parts(dn, 0), True, False)
                mm3(bank[1 + t % 2], (hT[0:TAIL, 0, 1, at], hT[0:TAIL, 1, 1, at]), (dn[0:TAIL, 0, 1], dn[0:TAIL, 1, 1]),
                    False, True).then_inc(S["down_made"], 1)

        quads(body)


def routing_constants(nc, a, sem, m):
    made, bias_in = sem("routing_made"), sem("bias_in")
    with nc.Block() as block:
        @block.sync
        def _(sp):
            sp.dma_start(m["bias_row"][:], a["e_bias"].rearrange("(o n) -> o n", o=1).to_broadcast([P, EXPERTS])).then_inc(bias_in, 16)
            sp.wait_ge(bias_in, 16)

        @block.gpsimd
        def _(pool):
            nc.gpsimd.memset(m["seen"][:], 0.0)
            nc.gpsimd.memset(m["ones"][:], 1.0)
            nc.gpsimd.memset(m["before"][:], 0.0).then_inc(made, 1)
            nc.gpsimd.memset(m["lower"][:], 1.0).then_inc(made, 1)
            nc.gpsimd.iota(m["number"][:], pattern=[[1, EXPERTS]], base=0, channel_multiplier=0, allow_small_or_imprecise_dtypes=True)
            nc.gpsimd.iota(m["number2"][:], pattern=[[2, EXPERTS]], base=0, channel_multiplier=0, allow_small_or_imprecise_dtypes=True)
            nc.gpsimd.iota(m["token"][:], pattern=[[P, QUAD]], base=0, channel_multiplier=1, allow_small_or_imprecise_dtypes=True)
            pool.wait_ge(made, 2)
            nc.gpsimd.affine_select(out=m["before"][:], in_=m["before"][:], compare_op=ALU.is_ge, fill=1.0, base=0,
                                    pattern=[[-1, P]], channel_multiplier=1)
            nc.gpsimd.affine_select(out=m["lower"][:], in_=m["lower"][:], compare_op=ALU.is_gt, fill=0.0, base=0,
                                    pattern=[[1, EGROUPS], [-1, EGROUPS]], channel_multiplier=0)


def experts(nc, a, sem, sb, st, mm3, m):
    ident, psT, psX, psS = m["ident"], m["psT"], m["psX"], m["psS"]
    tails = [psS[:, 0, 0:CAP], psS[:, 0, BANK:BANK + CAP]]
    outs = [psS[:, 1, 0:BANK], psS[:, 1, BANK:2 * BANK]]
    hold = holder(sem)
    two = range(2)
    table = sb(st, "table_sb", [P, EXPERTS, CHALF, 2], I32)
    take = [sb(st, f"take{i}", [P, CHALF, 2], I32) for i in two]
    give = [sb(st, f"give{i}", [P, CHALF, 2], I32) for i in two]
    rows = [sb(st, f"rows{i}", [P, CHALF, DIM]) for i in two]
    rowsT = [sb(st, f"rowsT{i}", [P, 2, CHUNKS, CAP], F32R) for i in two]
    gu_raw = [sb(st, f"gu_raw{i}", [P, CHUNKS, 2, INNER]) for i in two]
    dn_raw = [sb(st, f"dn_raw{i}", [P, 2, DIM]) for i in two]
    gu = [sb(st, f"gu{i}", [P, 2, CHUNKS, GU], F32R) for i in two]
    dn = [sb(st, f"dn{i}", [P, 2, 2, DIM], F32R) for i in two]
    gate = sb(st, "gate_e", [P, 2, CAP])
    inner = sb(st, "inner_e", [P, 2, CAP])
    hT = [sb(st, f"hT{i}", [P, 2, 2, CAP], F32R) for i in two]
    y = [sb(st, f"y{i}", [P, CHALF, DIM]) for i in two]
    names = ("table_in", "take_set", "give_set", "turned", "turned_high", "turned_low", "gu_high", "gu_low", "dn_high",
             "dn_low", "gated", "silu_made", "inner_made", "inner_high", "inner_low", "down_made", "y_made", "added", "pads")
    S = {n: sem("e_" + n) for n in names}
    gathered = [sem("e_gathered0"), sem("e_gathered1")]
    gu_in = [sem("e_gu_in0"), sem("e_gu_in1")]
    dn_in = [sem("e_dn_in0"), sem("e_dn_in1")]
    block = st.enter_context(nc.Block())

    def every(body, peeled=2):
        def run(eng):
            for e in range(peeled):
                body(e, e % 2, e // 2, e == 0, False)
            with eng.Fori(peeled // 2, EXPERTS // 2 - 1) as i:
                body(2 * i, 0, i, False, False)
                body(2 * i + 1, 1, i, False, False)
            body(EXPERTS - 2, 0, EXPERTS // 2 - 1, False, False)
            body(EXPERTS - 1, 1, EXPERTS // 2 - 1, False, True)
        return run

    @block.sync
    def _(sp):
        sp.dma_start(table[:].rearrange("p e h w -> p (e h) w"), m["slot_table"].rearrange("(p n) w -> p n w", p=P)).then_inc(S["table_in"], 16)

        def load_gu(e, k):
            if not (isinstance(e, int) and e < 2):
                hold(sp, S["gu_low"], 2 * e - 2)
            for w, name in enumerate(("w_gate", "w_up")):
                sp.dma_start(gu_raw[k][:, :, w, :], a[name][bass.ds(e, 1)].squeeze(0).rearrange("(c p) n -> p c n", p=P)).then_inc(gu_in[k], 16)

        def load_dn(e, k):
            if not (isinstance(e, int) and e < 2):
                hold(sp, S["dn_low"], e - 1)
            down = a["w_down"][bass.ds(e, 1)].squeeze(0)
            sp.dma_start(dn_raw[k][:, 0, :], down[0:P, :]).then_inc(dn_in[k], 16)
            sp.dma_start(dn_raw[k][0:TAIL, 1, :], down[P:INNER, :]).then_inc(dn_in[k], 16)

        load_gu(0, 0)
        load_gu(1, 1)
        sp.wait_ge(S["pads"], 5)
        load_dn(0, 0)
        load_dn(1, 1)
        load_gu(2, 0)
        with sp.Fori(0, EXPERTS // 2 - 2) as i:
            for k in range(2):
                load_gu(2 * i + k + 3, 1 - k)
                load_dn(2 * i + k + 2, k)
        load_gu(EXPERTS - 1, 1)
        load_dn(EXPERTS - 2, 0)
        load_dn(EXPERTS - 1, 1)

    @block.gpsimd
    def _(pool):
        def gather(e, k, opening=False):
            if not opening:
                hold(pool, S["turned"], CHALF * (e - 2) + CHALF)
            at = bass.ds(e, 1)
            nc.gpsimd.tensor_copy(take[k][:], table[:, at].squeeze(1)).then_inc(S["take_set"], 1)
            hold(pool, S["take_set"], e + 1)
            for h in range(CHALF):
                nc.gpsimd.indirect_dma_start(rows[k][:, h, :], None, m["xn_rows"],
                                             bass.IndirectOffsetOnAxis(take[k][:, h, 0:1], 0)).then_inc(gathered[k], 16)

        def set_give(e, k):
            if not (isinstance(e, int) and e < 2):
                hold(pool, S["added"], 16 * CHALF * (e - 1))
            nc.gpsimd.tensor_copy(give[k][:], table[:, bass.ds(e, 1)].squeeze(1)).then_inc(S["give_set"], 1)

        def scatter(e, k):
            hold(pool, S["y_made"], CHALF * e + CHALF)
            for h in range(CHALF):
                nc.gpsimd.indirect_dma_start(m["sum_rows"], bass.IndirectOffsetOnAxis(give[k][:, h, 0:1], 0),
                                             y[k][:, h, :], None, compute_op=ALU.add).then_inc(S["added"], 16)

        def body(e, k, o, first, last):
            if not first:
                set_give(e - 1, 1 - k)
            if not (isinstance(e, int) and e + 2 >= EXPERTS):
                gather(e + 2, k)
            if not (isinstance(e, int) and e < 2):
                scatter(e - 2, k)

        pool.wait_ge(S["table_in"], 16)
        gather(0, 0, True)
        gather(1, 1, True)
        every(body, 4)(pool)
        set_give(EXPERTS - 1, 1)
        scatter(EXPERTS - 2, 0)
        pool.wait_ge(S["added"], 16 * CHALF * (EXPERTS - 1))
        scatter(EXPERTS - 1, 1)
        pool.wait_ge(S["added"], 16 * CHALF * EXPERTS)

    @block.scalar
    def _(act):
        def dn_high(e, k, o):
            act.wait_ge(dn_in[k], 32 * o + 32)
            if not (isinstance(e, int) and e < 2):
                act.wait_ge(S["down_made"], CHALF * (e - 2) + CHALF)
            nc.scalar.activation(dn[k][:, 0], dn_raw[k][:], ACT.Copy).then_inc(S["dn_high"], 1)

        def high_rows(e, k):
            for h in range(CHALF):
                act.wait_ge(S["turned"], CHALF * e + h + 1)
                nc.scalar.activation(rowsT[k][:, 0, :, h * P:(h + 1) * P], psT[h][:].rearrange("p (c n) -> p c n", n=P),
                                     ACT.Copy).then_inc(S["turned_high"], 1)

        def weighted(e, k):
            act.wait_ge(S["give_set"], e + 1)
            for h in range(CHALF):
                act.wait_ge(S["down_made"], CHALF * e + h + 1)
                nc.scalar.activation(y[k][:, h, :], outs[h], ACT.Copy, scale=give[k][:, h, 1:2].bitcast(F32)).then_inc(S["y_made"], 1)

        def body(e, k, o, first, last):
            dn_high(e, k, o)
            if not last:
                high_rows(e + 1, 1 - k)
            act.wait_ge(S["gated"], 2 * e + 2)
            nc.scalar.activation(gate[:, 0], psX[k][:, 0:CAP], ACT.Silu).then_inc(S["silu_made"], 1)
            nc.scalar.activation(gate[0:TAIL, 1], tails[k][0:TAIL], ACT.Silu).then_inc(S["silu_made"], 1)
            act.wait_ge(S["inner_made"], 2 * e + 2)
            nc.scalar.activation(hT[k][:, 0], inner[:], ACT.Copy).then_inc(S["inner_high"], 1)
            if not first:
                weighted(e - 1, 1 - k)

        high_rows(0, 0)
        every(body)(act)
        weighted(EXPERTS - 1, 1)

    @block.vector
    def _(dve):
        def split_gu(e, k, o):
            dve.wait_ge(gu_in[k], 32 * o + 32)
            if not (isinstance(e, int) and e < 2):
                dve.wait_ge(S["gated"], 2 * (e - 2) + 2)
            highs, lows = gu_views(gu[k][:, 0], gu_raw[k]), gu_views(gu[k][:, 1], gu_raw[k])
            for high, raw in highs:
                nc.vector.tensor_copy(high, raw).then_inc(S["gu_high"], 1)
            for i, ((low, raw), (high, _)) in enumerate(zip(lows, highs)):
                dve.wait_ge(S["gu_high"], 2 * e + i + 1)
                nc.vector.tensor_tensor(low, raw, high.bitcast(F32), ALU.subtract).then_inc(S["gu_low"], 1)

        def dn_low(e, k):
            dve.wait_ge(S["dn_high"], e + 1)
            nc.vector.tensor_tensor(dn[k][:, 1], dn_raw[k][:], dn[k][:, 0].bitcast(F32), ALU.subtract).then_inc(S["dn_low"], 1)

        def low_rows(e, k):
            for h in range(CHALF):
                dve.wait_ge(S["turned_high"], CHALF * e + h + 1)
                at = (slice(None), slice(None), slice(h * P, (h + 1) * P))
                nc.vector.tensor_tensor(rowsT[k][:, 1][at], psT[h][:].rearrange("p (c n) -> p c n", n=P),
                                        rowsT[k][:, 0][at].bitcast(F32), ALU.subtract).then_inc(S["turned_low"], 1)

        def body(e, k, o, first, last):
            if not last:
                split_gu(e + 1, 1 - k, o + k)
                low_rows(e + 1, 1 - k)
            dn_low(e, k)
            if not first:
                dve.wait_ge(S["inner_low"], e)
            dve.wait_ge(S["silu_made"], 2 * e + 2)
            nc.vector.tensor_tensor(inner[:, 0], gate[:, 0], psX[k][:, CAP:2 * CAP], ALU.mult).then_inc(S["inner_made"], 1)
            nc.vector.tensor_tensor(inner[0:TAIL, 1], gate[0:TAIL, 1], tails[k][64:64 + TAIL], ALU.mult).then_inc(S["inner_made"], 1)
            dve.wait_ge(S["inner_high"], e + 1)
            nc.vector.tensor_tensor(hT[k][:, 1], inner[:], hT[k][:, 0].bitcast(F32), ALU.subtract).then_inc(S["inner_low"], 1)

        nc.vector.memset(inner[:], 0.0).then_inc(S["pads"], 1)
        for k in range(2):
            nc.vector.memset(gu[k][:].bitcast(F32), 0.0).then_inc(S["pads"], 1)
            nc.vector.memset(dn_raw[k][:, 1], 0.0).then_inc(S["pads"], 1)
        dve.wait_ge(S["pads"], 5)
        split_gu(0, 0, 0)
        low_rows(0, 0)
        every(body)(dve)

    @block.tensor
    def _(pe):
        def parts(x, *at):
            return x[(slice(None), 0) + at], x[(slice(None), 1) + at]

        def turn(e, k, o):
            pe.wait_ge(gathered[k], 16 * CHALF * (o + 1))
            for h in range(CHALF):
                if not (isinstance(e, int) and e == 0):
                    pe.wait_ge(S["turned_low"], CHALF * (e - 1) + h + 1)
                for c in range(CHUNKS):
                    last = nc.tensor.transpose(psT[h][:, c * P:(c + 1) * P], rows[k][:, h, c * P:(c + 1) * P], ident[:])
                last.then_inc(S["turned"], 1)

        def into(e, k, between=None):
            pe.wait_ge(S["gu_low"], 2 * e + 2)
            pe.wait_ge(S["turned_low"], CHALF * e + CHALF)
            if not (isinstance(e, int) and e < 2):
                pe.wait_ge(S["inner_made"], 2 * (e - 2) + 2)
            for w in range(2):
                for c in range(CHUNKS):
                    last = mm3(psX[k][:, w * CAP:(w + 1) * CAP], parts(gu[k], c, slice(w * P, (w + 1) * P)), parts(rowsT[k], c), c == 0, c == CHUNKS - 1)
                if w == 0 and between:
                    between()
            last.then_inc(S["gated"], 1)
            for c in range(CHUNKS):
                last = mm3(tails[k], parts(gu[k], c, slice(2 * P, GU)), parts(rowsT[k], c), c == 0, c == CHUNKS - 1)
            last.then_inc(S["gated"], 1)

        def down(e, k):
            pe.wait_ge(S["inner_low"], e + 1)
            pe.wait_ge(S["dn_low"], e + 1)
            for h in range(CHALF):
                if not (isinstance(e, int) and e == 0):
                    pe.wait_ge(S["y_made"], CHALF * (e - 1) + h + 1)
                at = slice(h * P, (h + 1) * P)
                mm3(outs[h], parts(hT[k], 0, at), parts(dn[k], 0), True, False)
                mm3(outs[h], (hT[k][0:TAIL, 0, 1, at], hT[k][0:TAIL, 1, 1, at]), (dn[k][0:TAIL, 0, 1], dn[k][0:TAIL, 1, 1]),
                    False, True).then_inc(S["down_made"], 1)

        def body(e, k, o, first, last):
            into(e, k, None if last else lambda: turn(e + 1, 1 - k, o + k))
            if not first:
                down(e - 1, 1 - k)

        turn(0, 0, 0)
        every(body)(pe)
        down(EXPERTS - 1, 1)


def finish(nc, sem, out, sum_rows):
    copied = sem("copied")
    with nc.Block() as block:
        @block.sync
        def _(sp):
            for b in range(BATCH):
                sp.dma_start(out[b].rearrange("(p r) d -> p (r d)", p=P),
                             sum_rows[b * SEQ:(b + 1) * SEQ, :].rearrange("(p r) d -> p (r d)", p=P)).then_inc(copied, 16)
            sp.wait_ge(copied, 16 * BATCH)


_NAMES = {
    "L0_attn_x": "x", "L0_attn_wq": "wq", "L0_attn_w_kv_down": "w_kv_down", "L0_attn_w_k_rope": "w_k_rope",
    "L0_attn_w_k_nope": "w_k_nope", "L0_attn_wv": "wv", "L0_attn_wo": "wo", "L0_attn_q_norm_w": "q_norm_w",
    "L0_attn_k_norm_w": "k_norm_w", "L0_ffn_router_weight": "router", "L0_ffn_e_bias": "e_bias",
    "L0_ffn_w_gate": "w_gate", "L0_ffn_w_up": "w_up", "L0_ffn_w_down": "w_down", "L0_ffn_sh_gate": "sh_gate",
    "L0_ffn_sh_up": "sh_up", "L0_ffn_sh_down": "sh_down"}


def kernel(**inputs):
    import numpy as np
    import concourse.bacc as bacc
    from concourse.bass_utils import run_bass_kernel_spmd

    nc = bacc.Bacc("TRN2", target_bir_lowering=False, num_devices=1)
    arrays, args = {}, {}
    for name, short in _NAMES.items():
        arrays[f"in_{short}"] = np.ascontiguousarray(inputs[name])
    freq = (np.float32(1.0 / 10000.0) ** np.linspace(0.0, 1.0, ROT, dtype=np.float32)).astype(np.float32)
    theta = np.arange(SEQ, dtype=np.float32)[:, None] * freq[None, :]
    arrays["in_rope_cos"], arrays["in_rope_sin"] = np.cos(theta), np.sin(theta)
    for name, array in arrays.items():
        args[name[3:]] = nc.dram_tensor(name, array.shape, F32, kind="ExternalInput").ap()
    out = nc.dram_tensor("out", (BATCH, SEQ, DIM), F32, kind="ExternalOutput").ap()
    build(nc, args, out)
    r = run_bass_kernel_spmd(nc, [arrays], core_ids=[0])
    return r.results[0]["out"]
```

```python
import concourse.bass as bass
from concourse import mybir
from contextlib import ExitStack

F32, F32R, BF16 = mybir.dt.float32, mybir.dt.float32r, mybir.dt.bfloat16
I32, U32 = mybir.dt.int32, mybir.dt.uint32
ACT = mybir.ActivationFunctionType
ALU = mybir.AluOpType
AX = mybir.AxisListType

P = 128
BANK = 512
BATCH, SEQ, DIM = 4, 1024, 512
HEADS, DK, DLAT, DROPE = 16, 128, 128, 64
TILES = SEQ // P
CHUNKS = DIM // P
PAIR = 2
GROUPS = HEADS // PAIR
GW = PAIR * DK
ROT = DROPE // 4
HALF = DROPE // 2
STEPS = PAIR * TILES
EPS_LN, EPS_RMS = 1e-5, 1e-6
MASKED = -1e30
TOKENS = BATCH * SEQ
EXPERTS, INNER, EGROUPS, TOPG, TOPK = 64, 176, 8, 4, 8
EG = EXPERTS // EGROUPS
CAP = 2 * 1024 * TOPK // EXPERTS
CHALF = CAP // P
SCALE_ROUTE = 2.5
TAIL = INNER - P
GU = 3 * P
QUAD = 4
QUADS = TILES // QUAD
CHOICES = TILES * TOPK
EARLY = 2 * TOPK
LATE = (CHOICES - EARLY) // GROUPS
SLOTS = EXPERTS * CAP
NEWTON = 3


def build(nc, a, out):
    def dram(name, shape, dt=F32):
        return nc.dram_tensor(name, shape, dt, kind="Internal").ap()

    wqk_split = dram("wqk_split", (GROUPS, P, 2, CHUNKS + 1, GW))
    wvo_split = dram("wvo_split", (GROUPS, P, 2, PAIR, DIM))
    xn_rows = dram("xn_rows", (TOKENS + CAP, DIM))
    sum_rows = dram("sum_rows", (TOKENS + CAP, DIM))
    slot_table = dram("slot_table", (SLOTS, 2), I32)

    outer = ExitStack()
    with outer:
        sems = {}

        def sem(name):
            if name not in sems:
                sems[name] = outer.enter_context(nc.semaphore(name))
            return sems[name]

        def sb(stack, name, shape, dt=F32):
            return stack.enter_context(nc.sbuf_tensor(name, shape, dt))

        ident = sb(outer, "ident", [P, P])
        ident_b = sb(outer, "ident_b", [P, P], BF16)
        kvd = sb(outer, "kvd", [P, 2, CHUNKS, DLAT], F32R)
        wq_col = sb(outer, "wq_col", [P, 1])
        newton = sb(outer, "newton", [P, 2])
        banks = [outer.enter_context(nc.psum_tensor(f"bank{i}", [P, BANK], F32)) for i in range(4)]
        psS = outer.enter_context(nc.psum_tensor("psS", [P, 2, 2 * BANK], F32))
        psT, psX = banks[0:2], banks[2:4]

        def mm3(dst, left, right, start, stop):
            (lh, ll), (rh, rl) = left, right
            nc.tensor.matmul(dst, lh, rh, start=start, stop=False)
            nc.tensor.matmul(dst, lh, rl, start=False, stop=False)
            return nc.tensor.matmul(dst, ll, rh, start=False, stop=stop)

        def rsqrt(dve, s, n, v, y, t, last=None):
            k = [0]

            def after(ins):
                k[0] += 1
                ins.then_inc(s, 1)
                dve.wait_ge(s, n + k[0])

            after(nc.vector.tensor_scalar(t.bitcast(I32), v.bitcast(I32), 1, None, ALU.logical_shift_right))
            after(nc.vector.tensor_scalar(y.bitcast(I32), t.bitcast(I32), -1.0, float(0x5F3759DF), ALU.mult, ALU.add))
            for _ in range(NEWTON):
                after(nc.vector.tensor_tensor(t, y, y, ALU.mult))
                after(nc.vector.scalar_tensor_tensor(t, t, -0.5, v, ALU.mult, ALU.mult))
                after(nc.vector.scalar_tensor_tensor(y, t, 1.5, y, ALU.add, ALU.mult))
            return k[0]

        RSQRT_OPS = 2 + 3 * NEWTON

        gu_split = dram("gu_split", (P, 2, CHUNKS, GU))
        dn_split = dram("dn_split", (P, 2, 2, DIM))
        rt_split = dram("rt_split", (P, 2, CHUNKS, EXPERTS))
        scratch = dict(nc=nc, xn_rows=xn_rows, sum_rows=sum_rows, slot_table=slot_table, gu_split=gu_split, dn_split=dn_split,
                       rt_split=rt_split,
                       table_row=sb(outer, "table_row", [P, CHOICES], I32),
                       entry=sb(outer, "entry", [P, CHOICES, 2], I32),
                       ident=ident, banks=banks, psT=psT, psX=psX, psS=psS)
        with ExitStack() as layers:
            acc = sb(layers, "acc", [P, TILES, DIM])
            rope = sb(layers, "rope", [P, 4, TILES, 2 * PAIR, ROT])
            causal = sb(layers, "causal", [P, P], BF16)
            routing = dict(
                scratch, acc=acc,
                seen=sb(layers, "seen", [P, EXPERTS], BF16),
                token=sb(layers, "token", [P, QUAD]),
                lower=sb(layers, "lower", [P, EGROUPS, EGROUPS]),
                before=sb(layers, "before", [P, P], BF16),
                ones=sb(layers, "ones", [P, P], BF16),
                number=sb(layers, "number", [P, EXPERTS]),
                number2=sb(layers, "number2", [P, EXPERTS]),
                bias_row=sb(layers, "bias_row", [P, EXPERTS]))
            with ExitStack() as st:
                with nc.Block() as block:
                    prepare(nc, a, sem, sb, st, block, dict(
                        ident=ident, ident_b=ident_b, kvd=kvd, wq_col=wq_col, newton=newton, wqk_split=wqk_split,
                        wvo_split=wvo_split, banks=banks, psS=psS))
                    rope_tables(nc, a, sem, sb, st, block, rope, causal)
                    routing_constants(nc, a, sem, block, routing)
                    split_ffn(nc, a, sem, sb, st, block, scratch)
            with nc.Fori(0, BATCH) as b:
                with ExitStack() as st:
                    attend(nc, a, b, sem, sb, st, mm3, rsqrt, RSQRT_OPS, dict(
                        ident=ident, ident_b=ident_b, kvd=kvd, wq_col=wq_col, newton=newton, wqk_split=wqk_split,
                        wvo_split=wvo_split, psT=psT, psX=psX, psS=psS, acc=acc, rope=rope, causal=causal, scratch=scratch))
                with ExitStack() as st:
                    route(nc, a, b, sem, sb, st, mm3, rsqrt, RSQRT_OPS, routing)
            with nc.Block() as block:
                @block.sync
                def _(sp):
                    for q in range(QUADS):
                        sp.wait_ge(sem(f"x_in{q}"), 16 * (BATCH + 1))
        with ExitStack() as st:
            experts(nc, a, sem, sb, st, mm3, scratch)
        finish(nc, sem, out, sum_rows)


def holder(sem):
    passed = sem("passed")

    def hold(eng, s, value):
        eng.wait_ge(s, value)
        if not isinstance(value, int):
            eng.sem_inc(passed, 1)
    return hold


def gu_views(part, raw):
    return [(part[:, :, 0:2 * P].rearrange("p c (w n) -> p c w n", w=2), raw[:, :, :, 0:P]),
            (part[:, :, 2 * P:GU].rearrange("p c (w n) -> p c w n", w=2)[:, :, :, 0:TAIL], raw[:, :, :, P:INNER])]


def prepare(nc, a, sem, sb, st, block, m):
    ident, ident_b, kvd, wq_col, banks = m["ident"], m["ident_b"], m["kvd"], m["wq_col"], m["banks"]
    ident_set, ident_b_set, kv_in, kv_high = sem("ident_set"), sem("ident_b_set"), sem("kv_in"), sem("kv_high")
    col_in, col_ones, col_set = sem("col_in"), sem("col_ones"), sem("col_set")
    wide_in = [sem("wide_in0"), sem("wide_in1")]
    wide_high, wide_low = sem("wide_high"), sem("wide_low")
    wide_out = [sem("wide_out0"), sem("wide_out1")]
    wv_in, wo_in = sem("wv_in"), [sem("wo_in0"), sem("wo_in1")]
    wv_turned, wv_copied, vo_made, vo_high, vo_low = sem("wv_turned"), sem("wv_copied"), sem("vo_made"), sem("vo_high"), sem("vo_low")
    vo_out = [sem("vo_out0"), sem("vo_out1")]
    wide = HEADS * DK
    def heads_of(c):
        return range(HEADS * c // (CHUNKS + 1), HEADS * (c + 1) // (CHUNKS + 1))

    kv_raw = sb(st, "kv_raw", [P, CHUNKS, DLAT])
    raw = sb(st, "raw", [P, 2, wide])
    part = sb(st, "part", [P, 2, 2, wide], F32R)
    cols = sb(st, "cols", [P, 2])
    wv_raw = sb(st, "wv_raw", [P, wide])
    wo_raw = sb(st, "wo_raw", [P, 2, DIM])
    wv_t = sb(st, "wv_t", [P, 2, DLAT])
    vo = sb(st, "vo", [P, 2, 2, DIM], F32R)

    @block.gpsimd
    def _(pool):
        nc.gpsimd.memset(ident[:], 0.0).then_inc(ident_set, 1)
        nc.gpsimd.memset(ident_b[:], 0.0).then_inc(ident_set, 1)
        nc.gpsimd.memset(m["newton"][:, 0:1], -0.5)
        nc.gpsimd.memset(m["newton"][:, 1:2], 1.5)
        pool.wait_ge(ident_set, 2)
        for i in (ident, ident_b):
            nc.gpsimd.affine_select(out=i[:], in_=i[:], compare_op=ALU.not_equal, fill=1.0, base=0,
                                    pattern=[[-1, P]], channel_multiplier=1).then_inc(ident_b_set, 1)

    @block.sync
    def _(sp):
        sp.dma_start(kv_raw[:], a["w_kv_down"].rearrange("(c p) n -> p c n", p=P)).then_inc(kv_in, 16)
        sp.dma_start(cols[:, 0:1], a["q_norm_w"].rearrange("(p o) -> p o", o=1)).then_inc(col_in, 16)
        sp.dma_start(cols[:, 1:2], a["k_norm_w"].rearrange("(p o) -> p o", o=1)).then_inc(col_in, 16)
        sp.dma_start(wv_raw[:], a["wv"]).then_inc(wv_in, 16)
        def load_chunk(c):
            k = c % 2
            if c >= 2:
                sp.wait_ge(wide_low, c - 1)
            if c < CHUNKS:
                sp.dma_start(raw[:, k, :], a["wq"][c * P:(c + 1) * P, :]).then_inc(wide_in[k], 16)
            else:
                r = raw[:, k, :].rearrange("p (h n) -> p h n", n=DK)
                sp.dma_start(r[:, :, 0:DROPE], a["w_k_rope"].rearrange("p (h n) -> p h n", n=DROPE)).then_inc(wide_in[k], 16)
                sp.dma_start(r[:, :, DROPE:DK], a["w_k_nope"].rearrange("p (h n) -> p h n", n=DK - DROPE)).then_inc(wide_in[k], 16)

        load_chunk(0)
        load_chunk(1)
        for c in range(CHUNKS + 1):
            for h in heads_of(c):
                if h >= 2:
                    sp.wait_ge(vo_made, h - 1)
                sp.dma_start(wo_raw[:, h % 2, :], a["wo"][h * DK:(h + 1) * DK, :]).then_inc(wo_in[h % 2], 16)
            if c + 2 <= CHUNKS:
                load_chunk(c + 2)

    @block.scalar
    def _(act):
        def copy_wv(h):
            k = h % 2
            act.wait_ge(wv_turned, h + 1)
            if h >= 2:
                act.wait_ge(vo_made, h - 1)
            nc.scalar.activation(wv_t[:, k, :], banks[k][:, 0:DLAT], ACT.Copy).then_inc(wv_copied, 1)

        copy_wv(0)
        act.wait_ge(kv_in, 16)
        nc.scalar.activation(kvd[:, 0, :, :], kv_raw[:], ACT.Copy).then_inc(kv_high, 1)
        for c in range(CHUNKS + 1):
            k = c % 2
            act.wait_ge(wide_in[k], 16 * (c // 2 + 1) + (16 if c == CHUNKS else 0))
            if c >= 2:
                act.wait_ge(wide_out[k], 32 * (c // 2))
            nc.scalar.activation(part[:, k, 0, :], raw[:, k, :], ACT.Copy).then_inc(wide_high, 1)
            act.wait_ge(wide_low, c + 1)
            act.wait_ge(wide_high, c + 1)
            for s in range(2):
                act.dma_start(m["wqk_split"][:, :, s, c, :].rearrange("g p n -> p g n"),
                              part[:, k, s, :].bitcast(F32).rearrange("p (g n) -> p g n", n=GW)).then_inc(wide_out[k], 16)
            for h in heads_of(c):
                k = h % 2
                if h + 1 < HEADS:
                    copy_wv(h + 1)
                act.wait_ge(vo_made, h + 1)
                if h >= 2:
                    act.wait_ge(vo_out[k], 16 * (h // 2))
                nc.scalar.activation(vo[:, k, 0, :], banks[2 + k][:], ACT.Copy).then_inc(vo_high, 1)
                act.wait_ge(vo_low, h + 1)
                act.dma_start(m["wvo_split"][h // PAIR, :, :, h % PAIR, :], vo[:, k, :, :].bitcast(F32)).then_inc(vo_out[k], 16)
        for k in range(2):
            act.wait_ge(wide_out[k], 32 * ((CHUNKS + 2 - k) // 2))
            act.wait_ge(vo_out[k], 16 * (HEADS // 2))

    @block.vector
    def _(dve):
        dve.wait_ge(kv_high, 1)
        nc.vector.tensor_tensor(kvd[:, 1, :, :], kv_raw[:], kvd[:, 0, :, :].bitcast(F32), ALU.subtract)
        dve.wait_ge(col_in, 32)
        nc.vector.memset(cols[0:ROT, 0:1], 1.0).then_inc(col_ones, 1)
        nc.vector.memset(cols[HALF:HALF + ROT, 0:1], 1.0).then_inc(col_ones, 1)
        dve.wait_ge(col_ones, 2)
        nc.vector.scalar_tensor_tensor(wq_col[:], cols[:, 0:1], float(DK) ** -0.5, cols[:, 1:2], ALU.mult, ALU.mult).then_inc(col_set, 1)
        for c in range(CHUNKS + 1):
            k = c % 2
            dve.wait_ge(wide_high, c + 1)
            nc.vector.tensor_tensor(part[:, k, 1, :], raw[:, k, :], part[:, k, 0, :].bitcast(F32),
                                    ALU.subtract).then_inc(wide_low, 1)
            for h in heads_of(c):
                k = h % 2
                dve.wait_ge(vo_high, h + 1)
                nc.vector.tensor_tensor(vo[:, k, 1, :], banks[2 + k][:], vo[:, k, 0, :].bitcast(F32),
                                        ALU.subtract).then_inc(vo_low, 1)

    @block.tensor
    def _(pe):
        pe.wait_ge(ident_b_set, 1)
        pe.wait_ge(wv_in, 16)
        def turn_wv(h):
            if h >= 2:
                pe.wait_ge(wv_copied, h - 1)
            nc.tensor.transpose(banks[h % 2][:, 0:DLAT], wv_raw[:, h * DK:(h + 1) * DK], ident[:]).then_inc(wv_turned, 1)

        turn_wv(0)
        for h in range(HEADS):
            k = h % 2
            if h + 1 < HEADS:
                turn_wv(h + 1)
            pe.wait_ge(wv_copied, h + 1)
            pe.wait_ge(wo_in[k], 16 * (h // 2 + 1))
            if h >= 2:
                pe.wait_ge(vo_low, h - 1)
            nc.tensor.matmul(banks[2 + k][:], wv_t[:, k, :], wo_raw[:, k, :], start=True, stop=True).then_inc(vo_made, 1)


def rope_tables(nc, a, sem, sb, st, block, rope, causal):
    trig_in, causal_set = sem("trig_in"), sem("causal_set")
    trig = sb(st, "trig", [P, 2, TILES, ROT])
    qw_row = sb(st, "qw_row", [P, DK])

    @block.sync
    def _(sp):
        sp.dma_start(trig[:, 0], a["rope_cos"].rearrange("(t p) n -> p t n", p=P)).then_inc(trig_in, 16)
        sp.dma_start(trig[:, 1], a["rope_sin"].rearrange("(t p) n -> p t n", p=P)).then_inc(trig_in, 16)
        sp.dma_start(qw_row[:], a["q_norm_w"].rearrange("(o n) -> o n", o=1).to_broadcast([P, DK])).then_inc(trig_in, 16)

    @block.vector
    def _(dve):
        dve.wait_ge(trig_in, 48)
        for table, which, first in ((0, 0, 0), (1, 1, HALF), (2, 0, HALF), (3, 1, 0)):
            w = qw_row[:, first:first + ROT].unsqueeze(1).to_broadcast([P, TILES, ROT])
            for slot in range(2 * PAIR):
                if slot < PAIR:
                    nc.vector.tensor_tensor(rope[:, table, :, slot, :], trig[:, which], w, ALU.mult)
                else:
                    nc.vector.tensor_copy(rope[:, table, :, slot, :], trig[:, which])

    @block.gpsimd
    def _(pool):
        nc.gpsimd.memset(causal[:], 0.0).then_inc(causal_set, 1)
        pool.wait_ge(causal_set, 1)
        nc.gpsimd.affine_select(out=causal[:], in_=causal[:], compare_op=ALU.is_ge, fill=MASKED, base=0,
                                pattern=[[-1, P]], channel_multiplier=1)


def attend(nc, a, b, sem, sb, st, mm3, rsqrt, RSQRT_OPS, m):
    ident, ident_b, kvd, wq_col = m["ident"], m["ident_b"], m["kvd"], m["wq_col"]
    psT, psX, psS, acc, rope, causal = m["psT"], m["psX"], m["psS"], m["acc"], m["rope"], m["causal"]
    hold = holder(sem)
    newton, scratch = m["newton"], m["scratch"]
    WIDTH = [5, 6, 7, 8]
    xnT = sb(st, "xnT", [P, 2, CHUNKS, SEQ], F32R)
    latT = sb(st, "latT", [P, 2, SEQ], F32R)
    lat = sb(st, "lat", [P, 2, TILES, DLAT], F32R)
    qk = sb(st, "qk", [P, TILES, 2 * PAIR, DK])
    sq = sb(st, "sq", [P, 2 * PAIR, DK])
    ss = sb(st, "ss", [P, TILES, 2 * PAIR])
    rn = sb(st, "rn", [P, TILES, 2 * PAIR])
    qT = sb(st, "qT", [P, 2, 2, SEQ], F32R)
    kT = sb(st, "kT", [P, 2, 2, SEQ], F32R)
    wqk = sb(st, "wqk", [P, 2, CHUNKS + 1, GW], F32R)
    wvo = sb(st, "wvo", [P, 2, PAIR, DIM], F32R)
    attnT = sb(st, "attnT", [P, 2, PAIR, SEQ], F32R)
    probs = [sb(st, f"probs{i}", [P, w * P]) for i, w in enumerate(WIDTH)]
    pT = [sb(st, f"pT{i}", [P, 2, 2 * (i + 1 + 2) , 2 * P], F32R) for i in range(2)]
    prod = sb(st, "prod", [P, 2, 4 * 2 * PAIR, ROT])
    newt = sb(st, "newt", [P, 3, 4 * 2 * PAIR])
    nmax = sb(st, "nmax", [P, 4])
    bias = sb(st, "bias", [P, 4])
    rsum = sb(st, "rsum", [P, 4])
    rinv = sb(st, "rinv", [P, 4])
    stats = sb(st, "stats", [P, TILES, 6])
    mv = sb(st, "mv", [P, TILES, 2])
    rstd = sb(st, "rstd", [P, TILES])
    late_row = sb(st, "late_row", [P, LATE], I32)
    late_entry = sb(st, "late_entry", [P, LATE, 2], I32)
    xn = [probs[2], probs[3]]

    x_in = [sem(f"x_in{i}") for i in range(QUADS)]
    S = {n: sem(n) for n in (
        "ln_stats", "ln_mean", "ln_var", "ln_rsqrt", "xn_made", "xn_turned", "xnT_high", "xnT_low",
        "lat_made", "latT_high", "latT_low", "lat_turned", "lat_high", "lat_low",
        "wqk_in", "wvo_in", "projected", "squared", "qk_copied", "sq_summed", "rope_prod", "rope_done",
        "ms_made", "ms_halved", "seeded", "newton_chain", "rn_made", "k_normed", "qk_turned", "qkT_high", "qkT_low",
        "scored", "max_made", "bias_made", "exped", "rinv_made", "normed", "p_turned", "pT_high", "pT_low",
        "valued", "attn_high", "attn_low", "rows_made", "rows_added", "late_copied", "late_scattered")}
    CHUNK = [0]
    for n in range(STEPS):
        CHUNK.append(CHUNK[-1] + (n % TILES) // 4 + 1)
    NCH = CHUNK[-1]
    OUT_AT = {t: [t] for t in range(TILES)}
    PROJ_AT = {6 + t: [t] for t in range(TILES)}
    TURN_AT = {0: (0, 0, 2), 2: (0, 0, 3), 4: (0, 1, 0), 6: (0, 1, 1), 8: (0, 1, 2), 10: (0, 1, 3), 12: (1, 0, 0), 14: (1, 0, 1)}
    LATE_AT = {3: 0, 4: 1, 5: 2, 8: 3, 11: 4, 15: 5}
    PAIRS = TILES // 2
    BANK_OF = {}
    for n in range(STEPS):
        tasks = [("values", (n // 2 - 1) % (2 * PAIRS))] if n % 2 else []
        tasks += [("rows", t) for t in OUT_AT.get(n, [])] + [("project", t) for t in PROJ_AT.get(n, [])]
        tasks += [("turn",) + TURN_AT[n][1:]] if n in TURN_AT else []
        for task in tasks:
            BANK_OF[task] = len(BANK_OF) % 2
    block = st.enter_context(nc.Block())

    def groups(eng, body):
        body(0, b * GROUPS, True, False)
        with eng.Fori(1, GROUPS - 1) as g:
            body(g, b * GROUPS + g, False, False)
        body(GROUPS - 1, b * GROUPS + (GROUPS - 1), False, True)

    @block.sync
    def _(sp):
        sp.dma_start(wqk[:].bitcast(F32), m["wqk_split"][0]).then_inc(S["wqk_in"], 16)

        def body(g, G, first, last):
            if not last:
                sp.wait_ge(S["projected"], (G + 1) * TILES)
                sp.dma_start(wqk[:].bitcast(F32), m["wqk_split"][bass.ds(g + 1, 1)].squeeze(0)).then_inc(S["wqk_in"], 16)
            if not first:
                sp.wait_ge(S["rows_made"], G * TILES)
            sp.dma_start(wvo[:].bitcast(F32), m["wvo_split"][bass.ds(g, 1)].squeeze(0)).then_inc(S["wvo_in"], 16)

        body(0, b * GROUPS, True, False)
        with sp.Fori(1, GROUPS - 1) as g:
            body(g, b * GROUPS + g, False, False)
        body(GROUPS - 1, b * GROUPS + (GROUPS - 1), False, True)

    @block.gpsimd
    def _(pool):
        def newton_steps(G, half):
            v, minus_half, t = newt[:, 0], newt[:, 2], newt[:, 1]
            y = rn[:, 4 * half:4 * half + 4].rearrange("p t s -> p (t s)")
            c = [newton[:, i:i + 1].to_broadcast([P, 4 * 2 * PAIR]) for i in range(2)]
            pool.wait_ge(S["seeded"], 2 * G + half + 1)
            ops = [(minus_half, v, c[0], ALU.mult)] + NEWTON * [
                (t, y, y, ALU.mult), (t, t, minus_half, ALU.mult), (t, t, c[1], ALU.add), (y, y, t, ALU.mult)]
            for i, (dst, left, right, op) in enumerate(ops):
                if i:
                    pool.wait_ge(S["newton_chain"], (2 * G + half) * (len(ops) - 1) + i)
                done = S["newton_chain"] if i + 1 < len(ops) else S["rn_made"]
                nc.gpsimd.tensor_tensor(dst, left, right, op).then_inc(done, 1)

        def norm_k(G, half):
            newton_steps(G, half)
            pool.wait_ge(S["rope_done"], 4 * G + 2 * half + 2)
            pool.wait_ge(S["rn_made"], 2 * G + half + 1)
            k = qk[:, 4 * half:4 * half + 4, PAIR:2 * PAIR, :]
            r = rn[:, 4 * half:4 * half + 4, PAIR:2 * PAIR].unsqueeze(3).to_broadcast([P, 4, PAIR, DK])
            nc.gpsimd.tensor_tensor(k, k, r, ALU.mult).then_inc(S["k_normed"], 1)

        def take_late(g, G, first):
            if not first:
                hold(pool, S["late_scattered"], G * (16 * LATE))
            nc.gpsimd.tensor_copy(late_row[:], scratch["table_row"][:, bass.ds(g * LATE + EARLY, LATE)]).then_inc(S["late_copied"], 1)
            nc.gpsimd.tensor_copy(late_entry[:], scratch["entry"][:, bass.ds(g * LATE + EARLY, LATE), :]).then_inc(S["late_copied"], 1)
            hold(pool, S["late_copied"], 2 * G + 2)

        def scatter_late(j):
            nc.gpsimd.indirect_dma_start(
                scratch["slot_table"], bass.IndirectOffsetOnAxis(late_row[:, j:j + 1], 0), late_entry[:, j, :], None,
                bounds_check=SLOTS - 1, oob_is_err=False).then_inc(S["late_scattered"], 16)

        def norm_p(G, n):
            t = n % TILES
            p = probs[n % 4][:, 0:(t + 1) * P]
            pool.wait_ge(S["rinv_made"], STEPS * G + n + 1)
            nc.gpsimd.tensor_tensor(p, p, rinv[:, n % 4:n % 4 + 1].to_broadcast([P, (t + 1) * P]), ALU.mult).then_inc(S["normed"], 1)

        def body(g, G, first, last):
            for n in range(STEPS):
                if n + 2 < STEPS:
                    norm_p(G, n + 2)
                elif not last:
                    norm_p(G + 1, n + 2 - STEPS)
                if n == 2:
                    take_late(g, G, first)
                if n in LATE_AT:
                    scatter_late(LATE_AT[n])
                if n == 9 and not last:
                    norm_k(G + 1, 0)
                if n == 13 and not last:
                    norm_k(G + 1, 1)

        norm_k(b * GROUPS, 0)
        norm_k(b * GROUPS, 1)
        norm_p(b * GROUPS, 0)
        norm_p(b * GROUPS, 1)
        groups(pool, body)
        hold(pool, S["late_scattered"], (b + 1) * (16 * LATE * GROUPS))

    @block.scalar
    def _(act):
        def copy_proj(G, t, bank, opening=False):
            act.wait_ge(S["projected"], TILES * G + t + 1)
            if not (opening and t == 0):
                act.wait_ge(S["sq_summed"], TILES * G + t)
            nc.scalar.activation(sq[:].rearrange("p s n -> p (s n)"), bank[:], ACT.Square).then_inc(S["squared"], 1)
            if not opening:
                act.wait_ge(S["qk_turned"], 2 * PAIRS * G - PAIRS + t // 2 + 1)
            nc.scalar.activation(qk[:, t].rearrange("p s n -> p (s n)"), bank[:], ACT.Copy).then_inc(S["qk_copied"], 1)

        def high_turned(G, h, pair):
            u = 2 * PAIRS * G + PAIRS * h + pair
            at = slice(2 * pair * P, (2 * pair + 2) * P)
            act.wait_ge(S["qk_turned"], u + 1)
            bank = psX[BANK_OF["turn", h, pair]]
            nc.scalar.activation(qT[:, h, 0, at], bank[:, 0:2 * P], ACT.Copy, scale=wq_col[:, 0:1]).then_inc(S["qkT_high"], 1)
            nc.scalar.activation(kT[:, h, 0, at], bank[:, 2 * P:4 * P], ACT.Copy).then_inc(S["qkT_high"], 1)

        def exp(G, n, opening=False):
            t = n % TILES
            act.wait_ge(S["bias_made"], STEPS * G + n + 1)
            if n >= 4:
                act.wait_ge(S["p_turned"], NCH * G + CHUNK[n - 3])
            elif not opening:
                act.wait_ge(S["p_turned"], NCH * G - NCH + CHUNK[n + 13])
            nc.scalar.activation(probs[n % 4][:, 0:(t + 1) * P], psS[:, n % 2, 0:(t + 1) * P], ACT.Exp,
                                 bias=bias[:, n % 4:n % 4 + 1], scale=rn[:, t, n // TILES:n // TILES + 1],
                                 accum_out=rsum[:, n % 4:n % 4 + 1]).then_inc(S["exped"], 1)

        def high_values(G, u):
            h, pair = u // PAIRS, u % PAIRS
            act.wait_ge(S["valued"], 2 * PAIRS * G + u + 1)
            nc.scalar.activation(attnT[:, 0, h, 2 * pair * P:(2 * pair + 2) * P], psX[BANK_OF["values", u]][:, 0:2 * P],
                                 ACT.Copy).then_inc(S["attn_high"], 1)

        def high_probs(G, n, opening):
            t = n % TILES
            u = n // 2
            if u >= 2:
                act.wait_ge(S["valued"], 2 * PAIRS * G + u - 1)
            elif not opening:
                act.wait_ge(S["valued"], 2 * PAIRS * G - 1 + u)
            for c in range(t // 4 + 1):
                act.wait_ge(S["p_turned"], NCH * G + CHUNK[n] + c + 1)
                k = min(4, t + 1 - 4 * c)
                nc.scalar.activation(pT[u % 2][:, 0, 4 * c:4 * c + k, (n % 2) * P:(n % 2 + 1) * P],
                                     psT[c][:, 0:k * P].rearrange("p (j q) -> p j q", q=P), ACT.Copy).then_inc(S["pT_high"], 1)

        def body(g, G, first, last):
            for n in range(STEPS):
                if n % 2 and not (first and n == 1):
                    high_values(G, n // 2 - 1) if n > 1 else high_values(G - 1, 2 * PAIRS - 1)
                for t in PROJ_AT.get(n, []) if not last else []:
                    copy_proj(G + 1, t, psX[BANK_OF["project", t]])
                if n in TURN_AT:
                    ahead, h, pair = TURN_AT[n]
                    if not (ahead and last):
                        high_turned(G + ahead, h, pair)
                high_probs(G, n, first)
                if n + 2 < STEPS:
                    exp(G, n + 2, first)
                elif not last:
                    exp(G + 1, n + 2 - STEPS)

        for t in range(TILES):
            act.wait_ge(S["xn_turned"], TILES * b + t + 1)
            nc.scalar.activation(xnT[:, 0, :, t * P:(t + 1) * P], psT[t % 2][:].rearrange("p (c q) -> p c q", q=P),
                                 ACT.Copy).then_inc(S["xnT_high"], 1)
        for q in range(2):
            act.wait_ge(S["lat_made"], 2 * b + q + 1)
            nc.scalar.activation(latT[:, 0, q * BANK:(q + 1) * BANK], psX[q][:], ACT.Copy).then_inc(S["latT_high"], 1)
        for q in range(2):
            act.wait_ge(S["lat_turned"], 4 * b + 2 * q + 1)
            nc.scalar.activation(lat[:, 0, 4 * q:4 * q + 4, :], psT[0][:].rearrange("p (j n) -> p j n", n=P),
                                 ACT.Copy).then_inc(S["lat_high"], 1)
        G0 = b * GROUPS
        for t in range(TILES):
            copy_proj(G0, t, psX[t % 2], opening=True)
        high_turned(G0, 0, 0)
        high_turned(G0, 0, 1)
        exp(G0, 0, opening=True)
        exp(G0, 1, opening=True)
        groups(act, body)
        high_values(G0 + (GROUPS - 1), 2 * PAIRS - 1)

    @block.vector
    def _(dve):
        def sum_squares(G, t):
            dve.wait_ge(S["squared"], TILES * G + t + 1)
            nc.vector.tensor_reduce(ss[:, t, :], sq[:], AX.X, ALU.add).then_inc(S["sq_summed"], 1)

        def rotate(G, half):
            dve.wait_ge(S["qk_copied"], TILES * G + 4 * half + 4)
            x = qk[:, 4 * half:4 * half + 4].rearrange("p t s n -> p (t s) n")
            x1, x2 = x[:, :, 0:ROT], x[:, :, HALF:HALF + ROT]
            tab = [rope[:, i, 4 * half:4 * half + 4].rearrange("p t s n -> p (t s) n") for i in range(4)]
            for dst, src, i in ((prod[:, 0], x2, 1), (prod[:, 1], x1, 3), (x1, x1, 0), (x2, x2, 2)):
                nc.vector.tensor_tensor(dst, src, tab[i], ALU.mult).then_inc(S["rope_prod"], 1)
            dve.wait_ge(S["rope_prod"], 8 * G + 4 * half + 4)
            nc.vector.tensor_tensor(x1, x1, prod[:, 0], ALU.add).then_inc(S["rope_done"], 1)
            nc.vector.tensor_tensor(x2, x2, prod[:, 1], ALU.subtract).then_inc(S["rope_done"], 1)

        def rms(G, half, opening=False):
            v, t = newt[:, 0], newt[:, 1]
            dve.wait_ge(S["sq_summed"], TILES * G + 4 * half + 4)
            if not (opening and half == 0):
                dve.wait_ge(S["rn_made"], 2 * G + half)
            nc.vector.tensor_scalar(v, ss[:, 4 * half:4 * half + 4].rearrange("p t s -> p (t s)"), 1.0 / DK, EPS_RMS,
                                    ALU.mult, ALU.add).then_inc(S["ms_made"], 1)
            dve.wait_ge(S["ms_made"], 2 * G + half + 1)
            nc.vector.tensor_scalar(t.bitcast(I32), v.bitcast(I32), 1, None, ALU.logical_shift_right).then_inc(S["ms_halved"], 1)
            if not opening:
                dve.wait_ge(S["exped"], STEPS * G - 4 + 4 * half)
                dve.wait_ge(S["k_normed"], 2 * G - 1 + half)
            dve.wait_ge(S["ms_halved"], 2 * G + half + 1)
            r = rn[:, 4 * half:4 * half + 4].rearrange("p t s -> p (t s)")
            nc.vector.tensor_scalar(r.bitcast(I32), t.bitcast(I32), -1.0, float(0x5F3759DF), ALU.mult,
                                    ALU.add).then_inc(S["seeded"], 1)

        def low_turned(G, h, pair):
            u = 2 * PAIRS * G + PAIRS * h + pair
            at = slice(2 * pair * P, (2 * pair + 2) * P)
            bank = psX[BANK_OF["turn", h, pair]]
            dve.wait_ge(S["qkT_high"], 2 * u + 2)
            nc.vector.scalar_tensor_tensor(qT[:, h, 1, at], bank[:, 0:2 * P], wq_col[:, 0:1], qT[:, h, 0, at].bitcast(F32),
                                           ALU.mult, ALU.subtract)
            nc.vector.tensor_tensor(kT[:, h, 1, at], bank[:, 2 * P:4 * P], kT[:, h, 0, at].bitcast(F32),
                                    ALU.subtract).then_inc(S["qkT_low"], 1)

        def row_max(G, n):
            t = n % TILES
            dve.wait_ge(S["scored"], STEPS * G + n + 1)
            nc.vector.tensor_reduce(nmax[:, n % 4:n % 4 + 1], psS[:, n % 2, 0:(t + 1) * P], AX.X, ALU.max,
                                    negate=True).then_inc(S["max_made"], 1)
            dve.wait_ge(S["max_made"], STEPS * G + n + 1)
            if n == 0:
                dve.wait_ge(S["rn_made"], 2 * G + 1)
            if n == 4:
                dve.wait_ge(S["rn_made"], 2 * G + 2)
            nc.vector.tensor_tensor(bias[:, n % 4:n % 4 + 1], nmax[:, n % 4:n % 4 + 1],
                                    rn[:, t, n // TILES:n // TILES + 1], ALU.mult).then_inc(S["bias_made"], 1)

        def invert(G, n):
            dve.wait_ge(S["exped"], STEPS * G + n + 1)
            nc.vector.reciprocal(rinv[:, n % 4:n % 4 + 1], rsum[:, n % 4:n % 4 + 1]).then_inc(S["rinv_made"], 1)

        def low_values(G, u):
            h, pair = u // PAIRS, u % PAIRS
            at = slice(2 * pair * P, (2 * pair + 2) * P)
            dve.wait_ge(S["attn_high"], 2 * PAIRS * G + u + 1)
            nc.vector.tensor_tensor(attnT[:, 1, h, at], psX[BANK_OF["values", u]][:, 0:2 * P], attnT[:, 0, h, at].bitcast(F32),
                                    ALU.subtract).then_inc(S["attn_low"], 1)

        def low_probs(G, n):
            t, u = n % TILES, n // 2
            for c in range(t // 4 + 1):
                dve.wait_ge(S["pT_high"], NCH * G + CHUNK[n] + c + 1)
                k = min(4, t + 1 - 4 * c)
                at = (slice(None), slice(4 * c, 4 * c + k), slice((n % 2) * P, (n % 2 + 1) * P))
                nc.vector.tensor_tensor(pT[u % 2][:, 1][at], psT[c][:, 0:k * P].rearrange("p (j q) -> p j q", q=P),
                                        pT[u % 2][:, 0][at].bitcast(F32), ALU.subtract).then_inc(S["pT_low"], 1)

        def add_rows(G, t, bank):
            dve.wait_ge(S["rows_made"], TILES * G + t + 1)
            nc.vector.tensor_tensor(acc[:, t, :], bank[:], acc[:, t, :], ALU.add).then_inc(S["rows_added"], 1)

        def body(g, G, first, last):
            for n in range(STEPS):
                if n + 2 < STEPS:
                    row_max(G, n + 2)
                elif not last:
                    row_max(G + 1, n + 2 - STEPS)
                if n % 2 and not (first and n == 1):
                    low_values(G, n // 2 - 1) if n > 1 else low_values(G - 1, 2 * PAIRS - 1)
                for t in OUT_AT.get(n, []) if not first else []:
                    add_rows(G - 1, t, psX[BANK_OF["rows", t]])
                for t in PROJ_AT.get(n, []) if not last else []:
                    sum_squares(G + 1, t)
                if n in TURN_AT:
                    ahead, h, pair = TURN_AT[n]
                    if not (ahead and last):
                        low_turned(G + ahead, h, pair)
                low_probs(G, n)
                if n + 2 < STEPS:
                    invert(G, n + 2)
                elif not last:
                    invert(G + 1, n + 2 - STEPS)
                if not last:
                    for at, half in ((9, 0), (13, 1)):
                        if n == at:
                            rms(G + 1, half)
                        if n == at + 1:
                            rotate(G + 1, half)

        for t in range(TILES):
            dve.wait_ge(x_in[t // QUAD], 16 * b + 16)
            nc.vector.bn_stats(stats[:, t, :], acc[:, t, :]).then_inc(S["ln_stats"], 1)
        for t in range(TILES):
            hold(dve, S["ln_stats"], TILES * b + t + 1)
            nc.vector.bn_aggr(mv[:, t, :], stats[:, t, :]).then_inc(S["ln_mean"], 1)
        dve.wait_ge(S["ln_mean"], TILES * b + TILES)
        nc.vector.tensor_scalar(newt[:, 0, 0:TILES], mv[:, :, 1], EPS_LN, None, ALU.add).then_inc(S["ln_var"], 1)
        dve.wait_ge(S["ln_var"], b + 1)
        rsqrt(dve, S["ln_rsqrt"], RSQRT_OPS * b, newt[:, 0, 0:TILES], rstd[:], newt[:, 1, 0:TILES])

        def normed_rows(t):
            if t >= 2:
                dve.wait_ge(S["xn_turned"], TILES * b + t - 1)
            nc.vector.tensor_scalar(xn[t % 2][:, 0:DIM], acc[:, t, :], mv[:, t, 0:1], rstd[:, t:t + 1],
                                    ALU.subtract, ALU.mult).then_inc(S["xn_made"], 1)

        normed_rows(0)
        for t in range(TILES):
            if t + 1 < TILES:
                normed_rows(t + 1)
            dve.wait_ge(S["xnT_high"], TILES * b + t + 1)
            at = (slice(None), slice(None), slice(t * P, (t + 1) * P))
            nc.vector.tensor_tensor(xnT[:, 1][at], psT[t % 2][:].rearrange("p (c q) -> p c q", q=P),
                                    xnT[:, 0][at].bitcast(F32), ALU.subtract).then_inc(S["xnT_low"], 1)
        for q in range(2):
            dve.wait_ge(S["latT_high"], 2 * b + q + 1)
            at = slice(q * BANK, (q + 1) * BANK)
            nc.vector.tensor_tensor(latT[:, 1, at], psX[q][:], latT[:, 0, at].bitcast(F32),
                                    ALU.subtract).then_inc(S["latT_low"], 1)
        for q in range(2):
            dve.wait_ge(S["lat_turned"], 4 * b + 2 * q + 2)
            nc.vector.tensor_copy(lat[:, 1, 4 * q:4 * q + 4, :],
                                  psT[1][:].rearrange("p (j n) -> p j n", n=P)).then_inc(S["lat_low"], 1)
        G0 = b * GROUPS
        for half in range(2):
            for t in range(4):
                sum_squares(G0, 4 * half + t)
            rms(G0, half, opening=True)
            rotate(G0, half)
        low_turned(G0, 0, 0)
        low_turned(G0, 0, 1)
        row_max(G0, 0)
        row_max(G0, 1)
        invert(G0, 0)
        invert(G0, 1)
        groups(dve, body)
        low_values(G0 + (GROUPS - 1), 2 * PAIRS - 1)
        for t in range(TILES):
            add_rows(G0 + (GROUPS - 1), t, psX[(t + 1) % 2])

    @block.tensor
    def _(pe):
        def parts(x, *at):
            return x[(slice(None), 0) + at], x[(slice(None), 1) + at]

        def project(G, t, bank, free):
            if t == 0:
                pe.wait_ge(S["wqk_in"], 16 * G + 16)
            if free:
                pe.wait_ge(*free)
            at = slice(t * P, (t + 1) * P)
            for c in range(CHUNKS):
                mm3(bank[:, 0:GW], parts(xnT, c, at), parts(wqk, c), c == 0, c == CHUNKS - 1)
            mm3(bank[:, GW:2 * GW], parts(latT, at), parts(wqk, CHUNKS), True, True).then_inc(S["projected"], 1)

        def turn(G, h, pair, free):
            if pair in (0, 2):
                pe.wait_ge(S["rope_done"], 4 * G + 2 * (pair // 2) + 2)
                pe.wait_ge(S["k_normed"], 2 * G + pair // 2 + 1)
            pe.wait_ge(*free)
            for i, (slot, j) in enumerate(((h, 0), (h, 1), (PAIR + h, 0), (PAIR + h, 1))):
                last = nc.tensor.transpose(psX[BANK_OF["turn", h, pair]][:, i * P:(i + 1) * P], qk[:, 2 * pair + j, slot, :], ident[:])
            last.then_inc(S["qk_turned"], 1)

        def score(G, n, opening=False):
            h, t = n // TILES, n % TILES
            if t % 2 == 0:
                pe.wait_ge(S["qkT_low"], 2 * PAIRS * G + PAIRS * h + t // 2 + 1)
            if not opening:
                pe.wait_ge(S["exped"], STEPS * G + n - 1)
            q = parts(qT[:, h], slice(t * P, (t + 1) * P))
            for first in range(0, t + 1, 4):
                at = slice(first * P, min(first + 4, t + 1) * P)
                diagonal = first + 4 > t
                last = mm3(psS[:, n % 2, at], q, parts(kT[:, h], at), True, not diagonal)
                if diagonal:
                    last = nc.tensor.matmul(psS[:, n % 2, t * P:(t + 1) * P], ident_b[:], causal[:], start=False, stop=True)
            last.then_inc(S["scored"], 1)

        def turn_probs(G, n, opening):
            t = n % TILES
            pe.wait_ge(S["normed"], STEPS * G + n + 1)
            for c in range(t // 4 + 1):
                if c == 0:
                    before = CHUNK[n - 1] + 1 if n else CHUNK[STEPS - 1] + 1 - NCH
                else:
                    before = CHUNK[n - 1] + 2 if t > 4 else (CHUNK[7] + 2 if n >= TILES else CHUNK[15] + 2 - NCH)
                if not (opening and before < 0 or opening and n == 0):
                    pe.wait_ge(S["pT_low"], NCH * G + before)
                for j in range(4 * c, min(4 * c + 4, t + 1)):
                    last = nc.tensor.transpose(psT[c][:, (j - 4 * c) * P:(j - 4 * c + 1) * P],
                                               probs[n % 4][:, j * P:(j + 1) * P], ident[:])
                last.then_inc(S["p_turned"], 1)

        def values(G, u, free):
            pair = u % PAIRS
            pe.wait_ge(S["pT_low"], NCH * G + CHUNK[2 * u + 2])
            pe.wait_ge(*free)
            for j in range(2 * pair + 2):
                at = slice(0, 2 * P) if j <= 2 * pair else slice(P, 2 * P)
                last = mm3(psX[BANK_OF["values", u]][:, at], parts(lat, j), parts(pT[u % 2], j, at), j == 0, j == 2 * pair + 1)
            last.then_inc(S["valued"], 1)

        def rows(G, t, bank, free):
            if t == 0:
                pe.wait_ge(S["wvo_in"], 16 * G + 16)
            if free[0] is not S["attn_low"]:
                pe.wait_ge(S["attn_low"], 2 * PAIRS * G + PAIRS + t // 2 + 1)
            pe.wait_ge(*free)
            for h in range(PAIR):
                last = mm3(bank[:], parts(attnT, h, slice(t * P, (t + 1) * P)), parts(wvo, h), h == 0, h == PAIR - 1)
            last.then_inc(S["rows_made"], 1)

        free = [None, None]

        def body(g, G, first, last):
            free[BANK_OF["turn", 0, 1]] = (S["qkT_low"], 2 * PAIRS * G + 2)
            free[1 - BANK_OF["turn", 0, 1]] = (S["qkT_low"], 2 * PAIRS * G + 1) if first else (S["attn_low"], 2 * PAIRS * G - 1)
            for n in range(STEPS):
                if n + 2 < STEPS:
                    score(G, n + 2)
                elif not last:
                    score(G + 1, n + 2 - STEPS)
                if n % 2 and not (first and n == 1):
                    of, u = (G, n // 2 - 1) if n > 1 else (G - 1, 2 * PAIRS - 1)
                    k = BANK_OF["values", u]
                    values(of, u, free[k])
                    free[k] = (S["attn_low"], 2 * PAIRS * of + u + 1)
                for t in OUT_AT.get(n, []) if not first else []:
                    k = BANK_OF["rows", t]
                    rows(G - 1, t, psX[k], free[k])
                    free[k] = (S["rows_added"], TILES * (G - 1) + t + 1)
                for t in PROJ_AT.get(n, []) if not last else []:
                    k = BANK_OF["project", t]
                    project(G + 1, t, psX[k], free[k])
                    free[k] = (S["qk_copied"], TILES * (G + 1) + t + 1)
                if n in TURN_AT:
                    ahead, h, pair = TURN_AT[n]
                    if not (ahead and last):
                        k = BANK_OF["turn", h, pair]
                        turn(G + ahead, h, pair, free[k])
                        free[k] = (S["qkT_low"], 2 * PAIRS * (G + ahead) + PAIRS * h + pair + 1)
                turn_probs(G, n, first)

        for t in range(TILES):
            pe.wait_ge(S["xn_made"], TILES * b + t + 1)
            if t >= 2:
                pe.wait_ge(S["xnT_low"], TILES * b + t - 1)
            for c in range(CHUNKS):
                last = nc.tensor.transpose(psT[t % 2][:, c * P:(c + 1) * P], xn[t % 2][:, c * P:(c + 1) * P], ident[:])
            last.then_inc(S["xn_turned"], 1)
        for q in range(2):
            pe.wait_ge(S["xnT_low"], TILES * b + 4 * q + 4)
            for c in range(CHUNKS):
                last = mm3(psX[q][:], parts(kvd, c), parts(xnT, c, slice(q * BANK, (q + 1) * BANK)), c == 0, c == CHUNKS - 1)
            last.then_inc(S["lat_made"], 1)
        for q in range(2):
            pe.wait_ge(S["latT_low"], 2 * b + q + 1)
            for part in range(2):
                if q:
                    pe.wait_ge(S["lat_high"] if part == 0 else S["lat_low"], 2 * b + 1)
                for j in range(4):
                    at = slice((4 * q + j) * P, (4 * q + j + 1) * P)
                    last = nc.tensor.transpose(psT[part][:, j * P:(j + 1) * P], latT[:, part, at].bitcast(F32), ident[:])
                last.then_inc(S["lat_turned"], 1)
        G0 = b * GROUPS
        for t in range(TILES):
            project(G0, t, psX[t % 2], (S["qk_copied"], TILES * G0 + t - 1) if t >= 2 else (S["latT_low"], 2 * b + t + 1))
        turn(G0, 0, 0, (S["qk_copied"], TILES * G0 + TILES))
        turn(G0, 0, 1, (S["qk_copied"], TILES * G0 + TILES))
        score(G0, 0, opening=True)
        score(G0, 1, opening=True)
        groups(pe, body)
        G = G0 + (GROUPS - 1)
        k = BANK_OF["values", 2 * PAIRS - 1]
        values(G, 2 * PAIRS - 1, free[k])
        free[k] = (S["attn_low"], 2 * PAIRS * G + 2 * PAIRS)
        for t in range(TILES):
            k = (t + 1) % 2
            rows(G, t, psX[k], free[k])
            free[k] = (S["rows_added"], TILES * G + t + 1)


def split_ffn(nc, a, sem, sb, st, block, m):
    ffn_in, ffn_high, ffn_low, ffn_out = sem("ffn_in"), sem("ffn_high"), sem("ffn_low"), sem("ffn_out")
    gu_raw = sb(st, "gu_raw", [P, CHUNKS, 2, INNER])
    dn_raw = sb(st, "dn_raw", [P, 2, DIM])
    rt_raw = sb(st, "rt_raw", [P, CHUNKS, EXPERTS])
    rt_rows = sb(st, "rt_rows", [EXPERTS, DIM])
    gu = sb(st, "gu_parts", [P, 2, CHUNKS, GU], F32R)
    dn = sb(st, "dn_parts", [P, 2, 2, DIM], F32R)
    rt = sb(st, "rt_parts", [P, 2, CHUNKS, EXPERTS], F32R)
    zero = sb(st, "zero", [P, DIM])
    table = sb(st, "table", [P, SLOTS // P, 2], I32)
    padded, turned, turned_out, zeroed, empty = sem("padded"), sem("rt_turned"), sem("rt_turned_copied"), sem("zeroed"), sem("table_empty")

    @block.sync
    def _(sp):
        sp.dma_start(rt_rows[:], a["router"]).then_inc(sem("rt_in"), 16)
        sp.wait_ge(padded, 2)
        sp.dma_start(gu_raw[:, :, 0, :], a["sh_gate"].rearrange("(c p) n -> p c n", p=P)).then_inc(ffn_in, 16)
        sp.dma_start(gu_raw[:, :, 1, :], a["sh_up"].rearrange("(c p) n -> p c n", p=P)).then_inc(ffn_in, 16)
        sp.dma_start(dn_raw[:, 0, :], a["sh_down"][0:P, :]).then_inc(ffn_in, 16)
        sp.dma_start(dn_raw[0:TAIL, 1, :], a["sh_down"][P:INNER, :]).then_inc(ffn_in, 16)
        sp.wait_ge(zeroed, 1)
        for i in range(CHALF):
            sp.dma_start(m["xn_rows"][TOKENS + i * P:TOKENS + (i + 1) * P, :], zero[:]).then_inc(ffn_out, 16)
            sp.dma_start(m["sum_rows"][TOKENS + i * P:TOKENS + (i + 1) * P, :], zero[:]).then_inc(ffn_out, 16)
        sp.wait_ge(empty, 2)
        sp.dma_start(m["slot_table"].rearrange("(p n) w -> p n w", p=P), table[:]).then_inc(ffn_out, 16)
        sp.wait_ge(ffn_low, 4)
        sp.dma_start(m["gu_split"], gu[:].bitcast(F32)).then_inc(ffn_out, 16)
        sp.dma_start(m["dn_split"], dn[:].bitcast(F32)).then_inc(ffn_out, 16)
        sp.dma_start(m["rt_split"], rt[:].bitcast(F32)).then_inc(ffn_out, 16)
        sp.wait_ge(ffn_out, 16 * (2 * CHALF + 4))

    @block.gpsimd
    def _(pool):
        nc.gpsimd.memset(gu[:].bitcast(F32), 0.0).then_inc(padded, 1)
        nc.gpsimd.memset(dn_raw[:], 0.0).then_inc(padded, 1)
        nc.gpsimd.memset(zero[:], 0.0).then_inc(zeroed, 1)
        nc.gpsimd.iota(table[:, :, 0].rearrange("p (e h) -> p e h", h=CHALF), pattern=[[0, EXPERTS], [P, CHALF]],
                       base=TOKENS, channel_multiplier=1).then_inc(empty, 1)
        nc.gpsimd.memset(table[:, :, 1], 0).then_inc(empty, 1)

    @block.tensor
    def _(pe):
        pe.wait_ge(sem("rt_in"), 16)
        for c in range(CHUNKS):
            last = nc.tensor.transpose(m["banks"][0][:, c * EXPERTS:(c + 1) * EXPERTS], rt_rows[:, c * P:(c + 1) * P],
                                       m["ident"][0:EXPERTS, 0:EXPERTS])
        last.then_inc(turned, 1)

    @block.scalar
    def _(act):
        act.wait_ge(turned, 1)
        nc.scalar.activation(rt_raw[:].rearrange("p c n -> p (c n)"), m["banks"][0][:, 0:CHUNKS * EXPERTS],
                             ACT.Copy).then_inc(turned_out, 1)
        act.wait_ge(turned_out, 1)
        nc.scalar.activation(rt[:, 0], rt_raw[:], ACT.Copy).then_inc(ffn_high, 1)
        act.wait_ge(ffn_in, 64)
        act.wait_ge(padded, 2)
        for dst, src in gu_views(gu[:, 0], gu_raw):
            nc.scalar.activation(dst, src, ACT.Copy).then_inc(ffn_high, 1)
        nc.scalar.activation(dn[:, 0], dn_raw[:], ACT.Copy).then_inc(ffn_high, 1)

    @block.vector
    def _(dve):
        dve.wait_ge(ffn_high, 1)
        nc.vector.tensor_tensor(rt[:, 1], rt_raw[:], rt[:, 0].bitcast(F32), ALU.subtract).then_inc(ffn_low, 1)
        for i, ((low, raw), (high, _)) in enumerate(zip(gu_views(gu[:, 1], gu_raw), gu_views(gu[:, 0], gu_raw))):
            dve.wait_ge(ffn_high, i + 2)
            nc.vector.tensor_tensor(low, raw, high.bitcast(F32), ALU.subtract).then_inc(ffn_low, 1)
        dve.wait_ge(ffn_high, 4)
        nc.vector.tensor_tensor(dn[:, 1], dn_raw[:], dn[:, 0].bitcast(F32), ALU.subtract).then_inc(ffn_low, 1)


def route(nc, a, b, sem, sb, st, mm3, rsqrt, RSQRT_OPS, m):
    ident, acc, psT, psX, psS = m["ident"], m["acc"], m["psT"], m["psX"], m["psS"]
    hold = holder(sem)
    W = QUAD * P
    bank = [psS[:, i // 2, (i % 2) * BANK:(i % 2 + 1) * BANK] for i in range(4)]
    gu = sb(st, "gu_sh", [P, 2, CHUNKS, GU], F32R)
    dn = sb(st, "dn_sh", [P, 2, 2, DIM], F32R)
    rt = sb(st, "rt_sh", [P, 2, CHUNKS, EXPERTS], F32R)
    stats = sb(st, "stats2", [P, QUAD, 6])
    mv = sb(st, "mv2", [P, QUAD, 2])
    var = sb(st, "var2", [P, QUAD])
    rstd = sb(st, "rstd2", [P, QUAD])
    temp = sb(st, "temp2", [P, QUAD])
    xn = sb(st, "xn2", [P, QUADS, QUAD, DIM])
    xnT = [sb(st, f"xnT2_{q}", [P, 2, CHUNKS, W], F32R) for q in range(QUADS)]
    gate = sb(st, "gate2", [P, 2, W])
    inner = sb(st, "inner2", [P, 2, W])
    hT = sb(st, "hT2", [P, 2, 2, W], F32R)
    base = sb(st, "base2", [P, QUAD, DIM])
    score = sb(st, "score2", [P, QUADS, QUAD, EXPERTS])
    biased = sb(st, "biased2", [P, QUAD, EXPERTS])
    hi4, lo4 = sb(st, "hi4", [P, QUAD * EGROUPS, 4]), sb(st, "lo4", [P, QUAD * EGROUPS, 4])
    hi2, lo2, mid2, low2 = [sb(st, n, [P, QUAD * EGROUPS, 2]) for n in ("hi2", "lo2", "mid2", "low2")]
    hi1, lo1, mid1, low1 = [sb(st, n, [P, QUAD * EGROUPS, 1]) for n in ("hi1", "lo1", "mid1", "low1")]
    gsum = sb(st, "gsum", [P, QUAD, EGROUPS])
    above = sb(st, "above", [P, QUAD, EGROUPS, EGROUPS])
    equal = sb(st, "equal", [P, QUAD, EGROUPS, EGROUPS])
    rank = sb(st, "rank", [P, QUAD, EGROUPS])
    keep = sb(st, "keep", [P, QUAD, EGROUPS])
    masked = sb(st, "masked", [P, QUAD, EXPERTS])
    replaced = sb(st, "replaced", [P, QUAD, EXPERTS])
    chosen = sb(st, "chosen", [P, QUADS, QUAD, EXPERTS], BF16)
    best = sb(st, "best", [P, QUAD, TOPK])
    expert = sb(st, "expert", [P, QUADS, QUAD, TOPK], U32)
    half = sb(st, "half", [P, QUAD, EXPERTS])
    row = sb(st, "row", [P, QUADS, QUAD, EXPERTS])
    onehot = sb(st, "onehot", [P, QUAD, TOPK, EXPERTS])
    prod_row = sb(st, "prod_row", [P, QUAD, TOPK, EXPERTS])
    prod_score = sb(st, "prod_score", [P, QUAD, TOPK, EXPERTS])
    row_f = sb(st, "row_f", [P, QUAD, TOPK])
    score_k = sb(st, "score_k", [P, QUAD, TOPK])
    score_sum = sb(st, "score_sum", [P, QUAD])
    table_row, entry = m["table_row"], m["entry"]
    seen, token, lower, before, ones, number, number2, bias_row = (
        m[k] for k in ("seen", "token", "lower", "before", "ones", "number", "number2", "bias_row"))
    x_in = [sem(f"x_in{i}") for i in range(QUADS)]
    names = ("ffn_w_in", "mean2", "var2", "rsqrt2", "xn2_made", "xn2_out", "xn2_turned", "xnT2_high", "xnT2_low",
             "logits", "scores_made", "chain", "chosen_made", "seen_made", "gated", "silu_made", "inner_made", "inner_high",
             "inner_low", "placed", "rows_ready", "onehot_made", "prods_made", "scored_made", "entries_made", "scattered",
             "down_made", "base_made", "base_out", "stats2_made")
    S = {n: sem("r_" + n) for n in names}
    block = st.enter_context(nc.Block())
    CHAIN = 54

    turn_bank = [bank[0], bank[1], bank[2], bank[3], bank[1], bank[2], bank[3], bank[1]]
    numbers = [(q, b * QUADS + q) for q in range(QUADS)]

    @block.sync
    def _(sp):
        sp.dma_start(gu[:].bitcast(F32), m["gu_split"]).then_inc(S["ffn_w_in"], 16)
        sp.dma_start(dn[:].bitcast(F32), m["dn_split"]).then_inc(S["ffn_w_in"], 16)
        sp.dma_start(rt[:].bitcast(F32), m["rt_split"]).then_inc(S["ffn_w_in"], 16)

        for q, Q in numbers:
            hold(sp, S["xn2_made"], Q * QUAD + QUAD)
            sp.dma_start(m["xn_rows"][bass.ds(Q * W, W), :].rearrange("(t p) d -> p t d", p=P), xn[:, q]).then_inc(S["xn2_out"], 16)
        for q, Q in numbers:
            hold(sp, S["base_made"], Q * QUAD + QUAD)
            sp.dma_start(m["sum_rows"][bass.ds(Q * W, W), :].rearrange("(t p) d -> p t d", p=P), base[:]).then_inc(S["base_out"], 16)
            load_x(sp, a, acc, (b + 1) % BATCH, q, x_in[q])
        hold(sp, S["xn2_out"], (b + 1) * (16 * QUADS))
        hold(sp, S["base_out"], (b + 1) * (16 * QUADS))

    @block.gpsimd
    def _(pool):
        for q, Q in numbers:
            for t in range(QUAD):
                hold(pool, S["onehot_made"], Q * QUAD + t + 1)
                nc.gpsimd.tensor_tensor(prod_row[:, t], onehot[:, t], row[:, q, t].unsqueeze(1).to_broadcast([P, TOPK, EXPERTS]),
                                        ALU.mult).then_inc(S["prods_made"], 1)
                if q == 0:
                    nc.gpsimd.tensor_tensor(prod_score[:, t], onehot[:, t], score[:, q, t].unsqueeze(1).to_broadcast([P, TOPK, EXPERTS]),
                                            ALU.mult).then_inc(S["scored_made"], 1)
            if q == 0:
                hold(pool, S["entries_made"], Q * 2 + 2)
                for i in range(EARLY):
                    scatter_choice(m, i, S["scattered"])
        hold(pool, S["scattered"], (b + 1) * (16 * EARLY))

    @block.scalar
    def _(act):
        def high_rows(q, Q):
            for t in range(QUAD):
                act.wait_ge(S["xn2_turned"], Q * QUAD + t + 1)
                nc.scalar.activation(xnT[q][:, 0, :, t * P:(t + 1) * P], turn_bank[q * QUAD + t].rearrange("p (c n) -> p c n", n=P),
                                     ACT.Copy).then_inc(S["xnT2_high"], 1)

        def scores(q, Q):
            act.wait_ge(S["logits"], Q + 1)
            nc.scalar.activation(score[:, q].rearrange("p t n -> p (t n)"), psT[q][:, 0:QUAD * EXPERTS],
                                 ACT.Sigmoid).then_inc(S["scores_made"], 1)

        def silus(q, Q):
            act.wait_ge(S["gated"], Q * 3 + 3)
            nc.scalar.activation(gate[:, 0], psX[0][:], ACT.Silu).then_inc(S["silu_made"], 1)
            nc.scalar.activation(gate[0:TAIL, 1], bank[0][0:TAIL], ACT.Silu).then_inc(S["silu_made"], 1)

        def high_inner(q, Q):
            act.wait_ge(S["inner_made"], Q * 2 + 2)
            nc.scalar.activation(hT[:, 0, 0], inner[:, 0], ACT.Copy).then_inc(S["inner_high"], 1)
            nc.scalar.activation(hT[0:TAIL, 0, 1], inner[0:TAIL, 1], ACT.Copy).then_inc(S["inner_high"], 1)

        first, second = numbers
        for stage, quad in ((high_rows, first), (scores, first), (silus, first), (high_rows, second), (high_inner, first),
                            (scores, second), (silus, second), (high_inner, second)):
            stage(*quad)

    @block.vector
    def _(dve):
        link = [0]

        def after(ins):
            link[0] += 1
            ins.then_inc(S["chain"], 1)
            hold(dve, S["chain"], b * CHAIN + link[0])

        def normed(q, Q):
            for t in range(QUAD):
                last = nc.vector.bn_stats(stats[:, t, :], acc[:, q * QUAD + t, :])
            after(last)
            for t in range(QUAD):
                last = nc.vector.bn_aggr(mv[:, t, :], stats[:, t, :])
            after(last)
            after(nc.vector.tensor_scalar(var[:], mv[:, :, 1], EPS_LN, None, ALU.add))
            rsqrt(dve, S["rsqrt2"], RSQRT_OPS * Q, var[:], rstd[:], temp[:])
            for t in range(QUAD):
                nc.vector.tensor_scalar(xn[:, q, t], acc[:, q * QUAD + t, :], mv[:, t, 0:1], rstd[:, t:t + 1],
                                        ALU.subtract, ALU.mult).then_inc(S["xn2_made"], 1)

        def low_rows(q, Q):
            for t in range(QUAD):
                dve.wait_ge(S["xnT2_high"], Q * QUAD + t + 1)
                at = (slice(None), slice(None), slice(t * P, (t + 1) * P))
                nc.vector.tensor_tensor(xnT[q][:, 1][at], turn_bank[q * QUAD + t].rearrange("p (c n) -> p c n", n=P),
                                        xnT[q][:, 0][at].bitcast(F32), ALU.subtract).then_inc(S["xnT2_low"], 1)

        def choose(q, Q):
            dve.wait_ge(S["scores_made"], Q + 1)
            after(nc.vector.tensor_tensor(biased[:], score[:, q], bias_row[:].unsqueeze(1).to_broadcast([P, QUAD, EXPERTS]), ALU.add))
            x = biased[:].rearrange("p t (g n) -> p (t g) n", n=EG)
            nc.vector.tensor_tensor(hi4[:], x[:, :, 0:4], x[:, :, 4:8], ALU.max)
            after(nc.vector.tensor_tensor(lo4[:], x[:, :, 0:4], x[:, :, 4:8], ALU.min))
            for h, l, n, h_, l_, mid, low in ((hi4, lo4, 2, hi2, lo2, mid2, low2), (hi2, lo2, 1, hi1, lo1, mid1, low1)):
                nc.vector.tensor_tensor(h_[:], h[:, :, 0:n], h[:, :, n:2 * n], ALU.max)
                nc.vector.tensor_tensor(mid[:], h[:, :, 0:n], h[:, :, n:2 * n], ALU.min)
                after(nc.vector.tensor_tensor(low[:], l[:, :, 0:n], l[:, :, n:2 * n], ALU.max))
                after(nc.vector.tensor_tensor(l_[:], mid[:], low[:], ALU.max))
            after(nc.vector.tensor_tensor(gsum[:].rearrange("p t g -> p (t g)"), hi1[:, :, 0], lo1[:, :, 0], ALU.add))
            full = [P, QUAD, EGROUPS, EGROUPS]
            other, own = gsum[:].unsqueeze(2).to_broadcast(full), gsum[:].unsqueeze(3).to_broadcast(full)
            nc.vector.tensor_tensor(above[:], other, own, ALU.is_gt)
            after(nc.vector.tensor_tensor(equal[:], other, own, ALU.is_equal))
            after(nc.vector.tensor_tensor(equal[:], equal[:], lower[:].unsqueeze(1).to_broadcast(full), ALU.mult))
            after(nc.vector.tensor_tensor(above[:], above[:], equal[:], ALU.add))
            after(nc.vector.tensor_reduce(rank[:], above[:], AX.X, ALU.add))
            after(nc.vector.tensor_scalar(keep[:], rank[:], float(TOPG), None, ALU.is_lt))
            after(nc.vector.tensor_tensor(masked[:].rearrange("p t (g n) -> p (t g) n", n=EG), x,
                                          keep[:].rearrange("p t g -> p (t g)").unsqueeze(2).to_broadcast([P, QUAD * EGROUPS, EG]), ALU.mult))
            after(nc.vector.tensor_scalar(masked[:], masked[:], 0.0, None, ALU.add))
            for t in range(QUAD):
                last = nc.vector.max(best[:, t], masked[:, t])
            after(last)
            for t in range(QUAD):
                nc.vector.max_index(expert[:, q, t], best[:, t], masked[:, t])
                last = nc.vector.match_replace(replaced[:, t], best[:, t], masked[:, t], MASKED)
            after(last)
            nc.vector.tensor_tensor(chosen[:, q], replaced[:], masked[:], ALU.not_equal).then_inc(S["chosen_made"], 1)

        def shared_inner(q, Q):
            dve.wait_ge(S["silu_made"], Q * 2 + 2)
            nc.vector.tensor_tensor(inner[:, 0], gate[:, 0], psX[1][:], ALU.mult).then_inc(S["inner_made"], 1)
            nc.vector.tensor_tensor(inner[0:TAIL, 1], gate[0:TAIL, 1], bank[0][64:64 + TAIL], ALU.mult).then_inc(S["inner_made"], 1)
            dve.wait_ge(S["inner_high"], Q * 2 + 2)
            nc.vector.tensor_tensor(hT[:, 1, 0], inner[:, 0], hT[:, 0, 0].bitcast(F32), ALU.subtract).then_inc(S["inner_low"], 1)
            nc.vector.tensor_tensor(hT[0:TAIL, 1, 1], inner[0:TAIL, 1], hT[0:TAIL, 0, 1].bitcast(F32), ALU.subtract).then_inc(S["inner_low"], 1)

        def slot_rows(q, Q):
            dve.wait_ge(S["placed"], Q + 1)
            slot = psT[q][:, 0:QUAD * EXPERTS].rearrange("p (t n) -> p t n", n=EXPERTS)
            after(nc.vector.tensor_scalar(half[:], slot, float(P), float(P * P - 1), ALU.is_ge, ALU.mult))
            after(nc.vector.scalar_tensor_tensor(row[:, q], slot, float(P), half[:], ALU.mult, ALU.subtract))
            after(nc.vector.tensor_tensor(row[:, q], row[:, q], number2[:].unsqueeze(1).to_broadcast([P, QUAD, EXPERTS]), ALU.add))
            nc.vector.tensor_reduce(half[:, 0], chosen[:, q].rearrange("p t n -> p n t"), AX.X, ALU.add).then_inc(S["seen_made"], 1)
            hold(dve, S["seen_made"], Q * 2 + 1)
            nc.vector.tensor_tensor(seen[:], seen[:], half[:, 0], ALU.add).then_inc(S["seen_made"], 1)

        def onehots(q, Q):
            full = [P, TOPK, EXPERTS]
            for t in range(QUAD):
                nc.vector.tensor_tensor(onehot[:, t], number[:].unsqueeze(1).to_broadcast(full),
                                        expert[:, q, t].unsqueeze(2).to_broadcast(full), ALU.is_equal).then_inc(S["onehot_made"], 1)

        def entries(q, Q):
            for t in range(QUAD) if q else ():
                nc.vector.tensor_tensor(prod_score[:, t], onehot[:, t], score[:, q, t].unsqueeze(1).to_broadcast([P, TOPK, EXPERTS]),
                                        ALU.mult).then_inc(S["scored_made"], 1)
            for t in range(QUAD):
                hold(dve, S["prods_made"], Q * QUAD + t + 1)
                hold(dve, S["scored_made"], Q * QUAD + t + 1)
                nc.vector.tensor_reduce(row_f[:, t], prod_row[:, t], AX.X, ALU.add)
                last = nc.vector.tensor_reduce(score_k[:, t], prod_score[:, t], AX.X, ALU.add)
            after(last)
            after(nc.vector.tensor_reduce(score_sum[:], score_k[:], AX.X, ALU.add))
            after(nc.vector.tensor_scalar(score_sum[:], score_sum[:], 1e-20, None, ALU.add))
            after(nc.vector.reciprocal(score_sum[:], score_sum[:]))
            after(nc.vector.tensor_scalar(score_sum[:], score_sum[:], SCALE_ROUTE, None, ALU.mult))
            own = slice(q * QUAD * TOPK, (q + 1) * QUAD * TOPK)
            quad_entry = entry[:, own].rearrange("p (t k) w -> p t k w", k=TOPK)
            nc.vector.tensor_tensor(quad_entry[:, :, :, 1].bitcast(F32), score_k[:], score_sum[:].unsqueeze(2).to_broadcast([P, QUAD, TOPK]), ALU.mult)
            nc.vector.tensor_copy(quad_entry[:, :, :, 0], token[:].unsqueeze(2).to_broadcast([P, QUAD, TOPK])).then_inc(S["entries_made"], 1)
            nc.vector.tensor_copy(table_row[:, own], row_f[:].rearrange("p t k -> p (t k)")).then_inc(S["entries_made"], 1)
            hold(dve, S["entries_made"], Q * 2 + 1)
            nc.vector.tensor_scalar(token[:], token[:], float(W), None, ALU.add)

        def bases(q, Q):
            if q:
                dve.wait_ge(S["base_out"], 16 * Q)
            for t in range(QUAD):
                dve.wait_ge(S["down_made"], Q * QUAD + t + 1)
                nc.vector.tensor_tensor(base[:, t], bank[2 + t % 2], acc[:, q * QUAD + t, :], ALU.add).then_inc(S["base_made"], 1)

        first, second = numbers
        for stage, quad in ((normed, first), (low_rows, first), (normed, second), (choose, first), (low_rows, second),
                            (shared_inner, first), (slot_rows, first), (onehots, first), (bases, first), (entries, first),
                            (choose, second), (shared_inner, second), (slot_rows, second), (onehots, second),
                            (bases, second), (entries, second)):
            stage(*quad)
        assert link[0] == CHAIN, link[0]

    @block.tensor
    def _(pe):
        def parts(x, *at):
            return x[(slice(None), 0) + at], x[(slice(None), 1) + at]

        def turn(q, Q):
            for t in range(QUAD):
                pe.wait_ge(S["xn2_made"], Q * QUAD + t + 1)
                if q * QUAD + t >= 7:
                    pe.wait_ge(S["xnT2_low"], Q * QUAD + t - 2)
                dst = turn_bank[q * QUAD + t]
                for c in range(CHUNKS):
                    last = nc.tensor.transpose(dst[:, c * P:(c + 1) * P], xn[:, q, t, c * P:(c + 1) * P], ident[:])
                last.then_inc(S["xn2_turned"], 1)

        def logits(q, Q):
            for t in range(QUAD):
                pe.wait_ge(S["xnT2_low"], Q * QUAD + t + 1)
                for c in range(CHUNKS):
                    last = mm3(psT[q][:, t * EXPERTS:(t + 1) * EXPERTS], parts(xnT[q], c, slice(t * P, (t + 1) * P)), parts(rt, c),
                               c == 0, c == CHUNKS - 1)
            last.then_inc(S["logits"], 1)

        def gated(q, Q):
            for dst, at in ((psX[0][:], slice(0, P)), (psX[1][:], slice(P, 2 * P)), (bank[0], slice(2 * P, GU))):
                for c in range(CHUNKS):
                    last = mm3(dst, parts(gu, c, at), parts(xnT[q], c), c == 0, c == CHUNKS - 1)
                last.then_inc(S["gated"], 1)

        def slots(q, Q):
            pe.wait_ge(S["chosen_made"], Q + 1)
            if q:
                pe.wait_ge(S["seen_made"], Q * 2)
            for t in range(QUAD):
                dst = psT[q][:, t * EXPERTS:(t + 1) * EXPERTS]
                nc.tensor.matmul(dst, before[:], chosen[:, q, t], start=True, stop=False)
                for earlier in range(t):
                    nc.tensor.matmul(dst, ones[:], chosen[:, q, earlier], start=False, stop=False)
                last = nc.tensor.matmul(dst, ones[:], seen[:], start=False, stop=True)
            last.then_inc(S["placed"], 1)

        def down(q, Q):
            pe.wait_ge(S["inner_low"], Q * 2 + 2)
            for t in range(QUAD):
                if t >= 2:
                    pe.wait_ge(S["base_made"], Q * QUAD + t - 1)
                elif q:
                    pe.wait_ge(S["base_made"], Q * QUAD)
                at = slice(t * P, (t + 1) * P)
                mm3(bank[2 + t % 2], parts(hT, 0, at), parts(dn, 0), True, False)
                mm3(bank[2 + t % 2], (hT[0:TAIL, 0, 1, at], hT[0:TAIL, 1, 1, at]), (dn[0:TAIL, 0, 1], dn[0:TAIL, 1, 1]),
                    False, True).then_inc(S["down_made"], 1)

        first, second = numbers
        turn(*first)
        pe.wait_ge(S["ffn_w_in"], b * 48 + 48)
        for stage, quad in ((logits, first), (gated, first), (turn, second), (logits, second), (slots, first), (down, first),
                            (gated, second), (slots, second), (down, second)):
            stage(*quad)


def load_x(sp, a, acc, batch, q, done):
    sp.dma_start(acc[:, q * QUAD:(q + 1) * QUAD, :],
                 a["x"][bass.ds(batch, 1)].squeeze(0).rearrange("(t p) d -> p t d", p=P)[:, q * QUAD:(q + 1) * QUAD, :]).then_inc(done, 16)


def scatter_choice(m, i, done):
    nc = m["nc"]
    nc.gpsimd.indirect_dma_start(
        m["slot_table"], bass.IndirectOffsetOnAxis(m["table_row"][:, i:i + 1], 0), m["entry"][:, i, :], None,
        bounds_check=SLOTS - 1, oob_is_err=False).then_inc(done, 16)


def routing_constants(nc, a, sem, block, m):
    made, bias_in = sem("routing_made"), sem("bias_in")
    @block.sync
    def _(sp):
        sp.dma_start(m["bias_row"][:], a["e_bias"].rearrange("(o n) -> o n", o=1).to_broadcast([P, EXPERTS])).then_inc(bias_in, 16)
        for q in range(QUADS):
            load_x(sp, a, m["acc"], 0, q, sem(f"x_in{q}"))
        sp.wait_ge(bias_in, 16)

    @block.gpsimd
    def _(pool):
        nc.gpsimd.memset(m["seen"][:], 0.0)
        nc.gpsimd.memset(m["ones"][:], 1.0)
        nc.gpsimd.memset(m["table_row"][:], SLOTS)
        nc.gpsimd.memset(m["entry"][:], 0)
        nc.gpsimd.memset(m["before"][:], 0.0).then_inc(made, 1)
        nc.gpsimd.memset(m["lower"][:], 1.0).then_inc(made, 1)
        nc.gpsimd.iota(m["number"][:], pattern=[[1, EXPERTS]], base=0, channel_multiplier=0, allow_small_or_imprecise_dtypes=True)
        nc.gpsimd.iota(m["number2"][:], pattern=[[2, EXPERTS]], base=0, channel_multiplier=0, allow_small_or_imprecise_dtypes=True)
        nc.gpsimd.iota(m["token"][:], pattern=[[P, QUAD]], base=0, channel_multiplier=1, allow_small_or_imprecise_dtypes=True)
        pool.wait_ge(made, 2)
        nc.gpsimd.affine_select(out=m["before"][:], in_=m["before"][:], compare_op=ALU.is_ge, fill=1.0, base=0,
                                pattern=[[-1, P]], channel_multiplier=1)
        nc.gpsimd.affine_select(out=m["lower"][:], in_=m["lower"][:], compare_op=ALU.is_gt, fill=0.0, base=0,
                                pattern=[[1, EGROUPS], [-1, EGROUPS]], channel_multiplier=0)


def experts(nc, a, sem, sb, st, mm3, m):
    ident, psT, psX, psS = m["ident"], m["psT"], m["psX"], m["psS"]
    tails = [psS[:, 0, 0:CAP], psS[:, 0, BANK:BANK + CAP]]
    outs = [psS[:, 1, 0:BANK], psS[:, 1, BANK:2 * BANK]]
    hold = holder(sem)
    two = range(2)
    table = sb(st, "table_sb", [P, EXPERTS, CHALF, 2], I32)
    take = [sb(st, f"take{i}", [P, CHALF, 2], I32) for i in two]
    give = [sb(st, f"give{i}", [P, CHALF, 2], I32) for i in two]
    rows = [sb(st, f"rows{i}", [P, CHALF, DIM]) for i in two]
    rowsT = [sb(st, f"rowsT{i}", [P, 2, CHUNKS, CAP], F32R) for i in two]
    gu_raw = [sb(st, f"gu_raw{i}", [P, CHUNKS, 2, INNER]) for i in two]
    dn_raw = [sb(st, f"dn_raw{i}", [P, 2, DIM]) for i in two]
    gu = [sb(st, f"gu{i}", [P, 2, CHUNKS, GU], F32R) for i in two]
    dn = [sb(st, f"dn{i}", [P, 2, 2, DIM], F32R) for i in two]
    gate = sb(st, "gate_e", [P, 2, CAP])
    inner = sb(st, "inner_e", [P, 2, CAP])
    hT = [sb(st, f"hT{i}", [P, 2, 2, CAP], F32R) for i in two]
    y = [sb(st, f"y{i}", [P, CHALF, DIM]) for i in two]
    names = ("table_full", "table_in", "take_set", "give_set", "turned", "turned_high", "turned_low", "gu_high", "gu_low", "dn_high",
             "dn_low", "gated", "silu_made", "inner_made", "inner_high", "inner_low", "down_made", "y_made", "added", "pads")
    S = {n: sem("e_" + n) for n in names}
    gathered = [sem("e_gathered0"), sem("e_gathered1")]
    gu_in = [sem("e_gu_in0"), sem("e_gu_in1")]
    dn_in = [sem("e_dn_in0"), sem("e_dn_in1")]
    block = st.enter_context(nc.Block())

    def every(body, peeled=2):
        def run(eng):
            for e in range(peeled):
                body(e, e % 2, e // 2, e == 0, False)
            with eng.Fori(peeled // 2, EXPERTS // 2 - 1) as i:
                body(2 * i, 0, i, False, False)
                body(2 * i + 1, 1, i, False, False)
            body(EXPERTS - 2, 0, EXPERTS // 2 - 1, False, False)
            body(EXPERTS - 1, 1, EXPERTS // 2 - 1, False, True)
        return run

    @block.sync
    def _(sp):
        def load_gu(e, k):
            if not (isinstance(e, int) and e < 2):
                hold(sp, S["gu_low"], 2 * e - 2)
            for w, name in enumerate(("w_gate", "w_up")):
                sp.dma_start(gu_raw[k][:, :, w, :], a[name][bass.ds(e, 1)].squeeze(0).rearrange("(c p) n -> p c n", p=P)).then_inc(gu_in[k], 16)

        def load_dn(e, k):
            if not (isinstance(e, int) and e < 2):
                hold(sp, S["dn_low"], e - 1)
            down = a["w_down"][bass.ds(e, 1)].squeeze(0)
            sp.dma_start(dn_raw[k][:, 0, :], down[0:P, :]).then_inc(dn_in[k], 16)
            sp.dma_start(dn_raw[k][0:TAIL, 1, :], down[P:INNER, :]).then_inc(dn_in[k], 16)

        load_gu(0, 0)
        load_gu(1, 1)
        sp.wait_ge(S["pads"], 5)
        load_dn(0, 0)
        load_dn(1, 1)
        sp.wait_ge(S["table_full"], 16 * (CHOICES - EARLY))
        sp.dma_start(table[:].rearrange("p e h w -> p (e h) w"), m["slot_table"].rearrange("(p n) w -> p n w", p=P)).then_inc(S["table_in"], 16)
        load_gu(2, 0)
        with sp.Fori(0, EXPERTS // 2 - 2) as i:
            for k in range(2):
                load_gu(2 * i + k + 3, 1 - k)
                load_dn(2 * i + k + 2, k)
        load_gu(EXPERTS - 1, 1)
        load_dn(EXPERTS - 2, 0)
        load_dn(EXPERTS - 1, 1)

    @block.gpsimd
    def _(pool):
        def gather(e, k, opening=False):
            if not opening:
                hold(pool, S["turned"], CHALF * (e - 2) + CHALF)
            at = bass.ds(e, 1)
            nc.gpsimd.tensor_copy(take[k][:], table[:, at].squeeze(1)).then_inc(S["take_set"], 1)
            hold(pool, S["take_set"], e + 1)
            for h in range(CHALF):
                nc.gpsimd.indirect_dma_start(rows[k][:, h, :], None, m["xn_rows"],
                                             bass.IndirectOffsetOnAxis(take[k][:, h, 0:1], 0)).then_inc(gathered[k], 16)

        def set_give(e, k):
            if not (isinstance(e, int) and e < 2):
                hold(pool, S["added"], 16 * CHALF * (e - 1))
            nc.gpsimd.tensor_copy(give[k][:], table[:, bass.ds(e, 1)].squeeze(1)).then_inc(S["give_set"], 1)

        def scatter(e, k):
            hold(pool, S["y_made"], CHALF * e + CHALF)
            for h in range(CHALF):
                nc.gpsimd.indirect_dma_start(m["sum_rows"], bass.IndirectOffsetOnAxis(give[k][:, h, 0:1], 0),
                                             y[k][:, h, :], None, compute_op=ALU.add).then_inc(S["added"], 16)

        def body(e, k, o, first, last):
            if not first:
                set_give(e - 1, 1 - k)
            if not (isinstance(e, int) and e + 2 >= EXPERTS):
                gather(e + 2, k)
            if not (isinstance(e, int) and e < 2):
                scatter(e - 2, k)

        for i in range(EARLY, CHOICES):
            scatter_choice(m, i, S["table_full"])
        pool.wait_ge(S["table_in"], 16)
        gather(0, 0, True)
        gather(1, 1, True)
        every(body, 4)(pool)
        set_give(EXPERTS - 1, 1)
        scatter(EXPERTS - 2, 0)
        pool.wait_ge(S["added"], 16 * CHALF * (EXPERTS - 1))
        scatter(EXPERTS - 1, 1)
        pool.wait_ge(S["added"], 16 * CHALF * EXPERTS)

    @block.scalar
    def _(act):
        def dn_high(e, k, o):
            act.wait_ge(dn_in[k], 32 * o + 32)
            if not (isinstance(e, int) and e < 2):
                act.wait_ge(S["down_made"], CHALF * (e - 2) + CHALF)
            nc.scalar.activation(dn[k][:, 0], dn_raw[k][:], ACT.Copy).then_inc(S["dn_high"], 1)

        def high_rows(e, k):
            for h in range(CHALF):
                act.wait_ge(S["turned"], CHALF * e + h + 1)
                nc.scalar.activation(rowsT[k][:, 0, :, h * P:(h + 1) * P], psT[h][:].rearrange("p (c n) -> p c n", n=P),
                                     ACT.Copy).then_inc(S["turned_high"], 1)

        def weighted(e, k):
            act.wait_ge(S["give_set"], e + 1)
            for h in range(CHALF):
                act.wait_ge(S["down_made"], CHALF * e + h + 1)
                nc.scalar.activation(y[k][:, h, :], outs[h], ACT.Copy, scale=give[k][:, h, 1:2].bitcast(F32)).then_inc(S["y_made"], 1)

        def body(e, k, o, first, last):
            dn_high(e, k, o)
            if not last:
                high_rows(e + 1, 1 - k)
            act.wait_ge(S["gated"], 2 * e + 2)
            nc.scalar.activation(gate[:, 0], psX[k][:, 0:CAP], ACT.Silu).then_inc(S["silu_made"], 1)
            nc.scalar.activation(gate[0:TAIL, 1], tails[k][0:TAIL], ACT.Silu).then_inc(S["silu_made"], 1)
            act.wait_ge(S["inner_made"], 2 * e + 2)
            nc.scalar.activation(hT[k][:, 0], inner[:], ACT.Copy).then_inc(S["inner_high"], 1)
            if not first:
                weighted(e - 1, 1 - k)

        high_rows(0, 0)
        every(body)(act)
        weighted(EXPERTS - 1, 1)

    @block.vector
    def _(dve):
        def split_gu(e, k, o):
            dve.wait_ge(gu_in[k], 32 * o + 32)
            if not (isinstance(e, int) and e < 2):
                dve.wait_ge(S["gated"], 2 * (e - 2) + 2)
            highs, lows = gu_views(gu[k][:, 0], gu_raw[k]), gu_views(gu[k][:, 1], gu_raw[k])
            for high, raw in highs:
                nc.vector.tensor_copy(high, raw).then_inc(S["gu_high"], 1)
            for i, ((low, raw), (high, _)) in enumerate(zip(lows, highs)):
                dve.wait_ge(S["gu_high"], 2 * e + i + 1)
                nc.vector.tensor_tensor(low, raw, high.bitcast(F32), ALU.subtract).then_inc(S["gu_low"], 1)

        def dn_low(e, k):
            dve.wait_ge(S["dn_high"], e + 1)
            nc.vector.tensor_tensor(dn[k][:, 1], dn_raw[k][:], dn[k][:, 0].bitcast(F32), ALU.subtract).then_inc(S["dn_low"], 1)

        def low_rows(e, k):
            for h in range(CHALF):
                dve.wait_ge(S["turned_high"], CHALF * e + h + 1)
                at = (slice(None), slice(None), slice(h * P, (h + 1) * P))
                nc.vector.tensor_tensor(rowsT[k][:, 1][at], psT[h][:].rearrange("p (c n) -> p c n", n=P),
                                        rowsT[k][:, 0][at].bitcast(F32), ALU.subtract).then_inc(S["turned_low"], 1)

        def body(e, k, o, first, last):
            if not last:
                split_gu(e + 1, 1 - k, o + k)
                low_rows(e + 1, 1 - k)
            dn_low(e, k)
            if not first:
                dve.wait_ge(S["inner_low"], e)
            dve.wait_ge(S["silu_made"], 2 * e + 2)
            nc.vector.tensor_tensor(inner[:, 0], gate[:, 0], psX[k][:, CAP:2 * CAP], ALU.mult).then_inc(S["inner_made"], 1)
            nc.vector.tensor_tensor(inner[0:TAIL, 1], gate[0:TAIL, 1], tails[k][64:64 + TAIL], ALU.mult).then_inc(S["inner_made"], 1)
            dve.wait_ge(S["inner_high"], e + 1)
            nc.vector.tensor_tensor(hT[k][:, 1], inner[:], hT[k][:, 0].bitcast(F32), ALU.subtract).then_inc(S["inner_low"], 1)

        nc.vector.memset(inner[:], 0.0).then_inc(S["pads"], 1)
        for k in range(2):
            nc.vector.memset(gu[k][:].bitcast(F32), 0.0).then_inc(S["pads"], 1)
            nc.vector.memset(dn_raw[k][:, 1], 0.0).then_inc(S["pads"], 1)
        dve.wait_ge(S["pads"], 5)
        split_gu(0, 0, 0)
        low_rows(0, 0)
        every(body)(dve)

    @block.tensor
    def _(pe):
        def parts(x, *at):
            return x[(slice(None), 0) + at], x[(slice(None), 1) + at]

        def turn(e, k, o):
            pe.wait_ge(gathered[k], 16 * CHALF * (o + 1))
            for h in range(CHALF):
                if not (isinstance(e, int) and e == 0):
                    pe.wait_ge(S["turned_low"], CHALF * (e - 1) + h + 1)
                for c in range(CHUNKS):
                    last = nc.tensor.transpose(psT[h][:, c * P:(c + 1) * P], rows[k][:, h, c * P:(c + 1) * P], ident[:])
                last.then_inc(S["turned"], 1)

        def into(e, k, between=None):
            pe.wait_ge(S["gu_low"], 2 * e + 2)
            pe.wait_ge(S["turned_low"], CHALF * e + CHALF)
            if not (isinstance(e, int) and e < 2):
                pe.wait_ge(S["inner_made"], 2 * (e - 2) + 2)
            for w in range(2):
                for c in range(CHUNKS):
                    last = mm3(psX[k][:, w * CAP:(w + 1) * CAP], parts(gu[k], c, slice(w * P, (w + 1) * P)), parts(rowsT[k], c), c == 0, c == CHUNKS - 1)
                if w == 0 and between:
                    between()
            last.then_inc(S["gated"], 1)
            for c in range(CHUNKS):
                last = mm3(tails[k], parts(gu[k], c, slice(2 * P, GU)), parts(rowsT[k], c), c == 0, c == CHUNKS - 1)
            last.then_inc(S["gated"], 1)

        def down(e, k):
            pe.wait_ge(S["inner_low"], e + 1)
            pe.wait_ge(S["dn_low"], e + 1)
            for h in range(CHALF):
                if not (isinstance(e, int) and e == 0):
                    pe.wait_ge(S["y_made"], CHALF * (e - 1) + h + 1)
                at = slice(h * P, (h + 1) * P)
                mm3(outs[h], parts(hT[k], 0, at), parts(dn[k], 0), True, False)
                mm3(outs[h], (hT[k][0:TAIL, 0, 1, at], hT[k][0:TAIL, 1, 1, at]), (dn[k][0:TAIL, 0, 1], dn[k][0:TAIL, 1, 1]),
                    False, True).then_inc(S["down_made"], 1)

        def body(e, k, o, first, last):
            into(e, k, None if last else lambda: turn(e + 1, 1 - k, o + k))
            if not first:
                down(e - 1, 1 - k)

        turn(0, 0, 0)
        every(body)(pe)
        down(EXPERTS - 1, 1)


def finish(nc, sem, out, sum_rows):
    copied = sem("copied")
    with nc.Block() as block:
        @block.sync
        def _(sp):
            for b in range(BATCH):
                sp.dma_start(out[b].rearrange("(p r) d -> p (r d)", p=P),
                             sum_rows[b * SEQ:(b + 1) * SEQ, :].rearrange("(p r) d -> p (r d)", p=P)).then_inc(copied, 16)
            sp.wait_ge(copied, 16 * BATCH)


_NAMES = {
    "L0_attn_x": "x", "L0_attn_wq": "wq", "L0_attn_w_kv_down": "w_kv_down", "L0_attn_w_k_rope": "w_k_rope",
    "L0_attn_w_k_nope": "w_k_nope", "L0_attn_wv": "wv", "L0_attn_wo": "wo", "L0_attn_q_norm_w": "q_norm_w",
    "L0_attn_k_norm_w": "k_norm_w", "L0_ffn_router_weight": "router", "L0_ffn_e_bias": "e_bias",
    "L0_ffn_w_gate": "w_gate", "L0_ffn_w_up": "w_up", "L0_ffn_w_down": "w_down", "L0_ffn_sh_gate": "sh_gate",
    "L0_ffn_sh_up": "sh_up", "L0_ffn_sh_down": "sh_down"}


def kernel(**inputs):
    import numpy as np
    import concourse.bacc as bacc
    from concourse.bass_utils import run_bass_kernel_spmd

    nc = bacc.Bacc("TRN2", target_bir_lowering=False, num_devices=1)
    arrays, args = {}, {}
    for name, short in _NAMES.items():
        arrays[f"in_{short}"] = np.ascontiguousarray(inputs[name])
    freq = (np.float32(1.0 / 10000.0) ** np.linspace(0.0, 1.0, ROT, dtype=np.float32)).astype(np.float32)
    theta = np.arange(SEQ, dtype=np.float32)[:, None] * freq[None, :]
    arrays["in_rope_cos"], arrays["in_rope_sin"] = np.cos(theta), np.sin(theta)
    for name, array in arrays.items():
        args[name[3:]] = nc.dram_tensor(name, array.shape, F32, kind="ExternalInput").ap()
    out = nc.dram_tensor("out", (BATCH, SEQ, DIM), F32, kind="ExternalOutput").ap()
    build(nc, args, out)
    r = run_bass_kernel_spmd(nc, [arrays], core_ids=[0])
    return r.results[0]["out"]
```
